# Optimizing a Trainium2 kernel written in Bass

```python
import numpy as np
import jax
import jax.numpy as jnp

def _softmax(x, axis=-1):
    return jax.nn.softmax(x, axis=axis)

def _gelu(x):
    return jax.nn.gelu(x, approximate=True)

def _silu(x):
    return jax.nn.silu(x)

def _sigmoid(x):
    return jax.nn.sigmoid(x)

def _layernorm(x, axis=-1, eps=1e-05):
    m = jnp.mean(x, axis=axis, keepdims=True)
    v = jnp.var(x, axis=axis, keepdims=True)
    return (x - m) / jnp.sqrt(v + eps)

def _scatter_add(tgt, idx, src, axis=0):
    return tgt.at[idx].add(src)

def _segment_sum(src, seg, n):
    return jax.ops.segment_sum(src, seg, n)
kernel_name = 'mk_adj_resnorm_d4_adj_r2_033fe9'

def setup_inputs(seed: int=0):
    np.random.seed(seed)
    _w = jnp.asarray

    def _rec_inputs():
        import jax
        import jax.numpy as jnp
        _gk = jax.random.key(seed)
        x = -0.000929 + 1 * jax.random.normal(jax.random.fold_in(_gk, 1), (4096, 128), jnp.float32)
        _w = (1.0 + jnp.arange(4096, dtype=jnp.float32)) ** (-0.5)
        _w = _w / _w.mean()
        _pij = jnp.clip(0.00195312 * _w[:, None] * _w[None, :], 0.0, 1.0)
        _a = jax.random.uniform(jax.random.fold_in(_gk, 2), (4096, 4096)) < _pij
        _a = jnp.logical_or(_a, jnp.eye(4096, dtype=bool))
        _af = _a.astype(jnp.float32)
        _af = _af * jax.random.uniform(jax.random.fold_in(_gk, 3), (4096, 4096), jnp.float32, 0.05, 1)
        adj = _af
        return (x, adj)
    x, adj = _rec_inputs()

    def _L0_gnn_setup():
        import jax, jax.numpy as jnp
        import numpy as np
        NEG_SLOPE = 0.01
        N_U, N_V = (4096, 4096)
        U_F, V_F = (128, 128)
        HIDS = [128, 128]
        NUM_ROUNDS = 3

        def _glorot(key, fan_in, fan_out):
            lim = np.sqrt(6.0 / (fan_in + fan_out)).astype(np.float32)
            return jax.random.uniform(key, (fan_in, fan_out), jnp.float32, -lim, lim)

        def _mlp(x, W1, b1, W2, b2, W3, b3):
            a = jax.nn.leaky_relu
            x = a(x @ W1 + b1, NEG_SLOPE)
            x = a(x @ W2 + b2, NEG_SLOPE)
            return a(x @ W3 + b3, NEG_SLOPE)
        key = jax.random.key(seed)
        ks = jax.random.split(key, 12)
        inp = {'u_node_feats': jax.random.normal(ks[0], (N_U, U_F), jnp.float32), 'v_node_feats': jax.random.normal(ks[1], (N_V, V_F), jnp.float32), 'uv_adj_mat': jax.random.uniform(ks[2], (N_V, N_U), jnp.float32), 'vu_adj_mat': jax.random.uniform(ks[3], (N_U, N_V), jnp.float32)}
        dims_uv = [U_F] + HIDS + [V_F]
        dims_vu = [V_F] + HIDS + [U_F]
        k = 4
        for tag, dims in (('uv', dims_uv), ('vu', dims_vu)):
            for i in range(3):
                inp[f'{tag}_W{i + 1}'] = _glorot(ks[k], dims[i], dims[i + 1])
                k += 1
                inp[f'{tag}_b{i + 1}'] = jnp.zeros((dims[i + 1],), jnp.float32)
        return inp
    _L0_gnn_all = _L0_gnn_setup()
    _L0_gnn_in = {k: v for k, v in _L0_gnn_all.items() if k in ('v_node_feats', 'uv_W1', 'uv_b1', 'uv_W2', 'uv_b2', 'uv_W3', 'uv_b3', 'vu_W1', 'vu_b1', 'vu_W2', 'vu_b2', 'vu_W3', 'vu_b3')}
    del _L0_gnn_all

    def _L1_gnn_setup():
        import jax, jax.numpy as jnp
        import numpy as np
        N = 4096
        IN_DIM = 128
        OUT_DIM = 128
        key = jax.random.key(seed)
        k1, k2, k3, k4 = jax.random.split(key, 4)
        X = jax.random.normal(k1, (N, IN_DIM), dtype=jnp.float32)
        A = jax.random.uniform(k2, (N, N), dtype=jnp.float32)
        limit = float(np.sqrt(6.0 / (IN_DIM + OUT_DIM)))
        W = jax.random.uniform(k3, (OUT_DIM, IN_DIM), dtype=jnp.float32, minval=-limit, maxval=limit)
        b = jnp.zeros((OUT_DIM,), dtype=jnp.float32)
        return {'X': X, 'A': A, 'W': W, 'b': b}
    _L1_gnn_all = _L1_gnn_setup()
    _L1_gnn_in = {k: v for k, v in _L1_gnn_all.items() if k in ('W', 'b')}
    del _L1_gnn_all

    def _L2_gnn_setup():
        import jax, jax.numpy as jnp
        import numpy as np
        N = 8192
        C = 128
        F = 128
        key = jax.random.key(seed)
        k1, k2, k3, k4 = jax.random.split(key, 4)
        X = jax.random.normal(k1, (N, C), dtype=jnp.float32)
        adj = jax.random.uniform(k2, (N, N), dtype=jnp.float32)
        W = jax.random.normal(k3, (C, F), dtype=jnp.float32) * 0.05
        b = jax.random.normal(k4, (F,), dtype=jnp.float32) * 0.05
        return {'X': X, 'adj': adj, 'W': W, 'b': b}
    _L2_gnn_all = _L2_gnn_setup()
    _L2_gnn_in = {k: v for k, v in _L2_gnn_all.items() if k in ('W', 'b')}
    del _L2_gnn_all

    def _L3_gnn_setup():
        import jax, jax.numpy as jnp
        import numpy as np
        N, E, D = (4096, 4096, 128)
        key = jax.random.key(seed)
        k1, k2 = jax.random.split(key)
        X = jax.random.normal(k1, (N, D), dtype=jnp.float32)
        H = jax.random.uniform(k2, (N, E), dtype=jnp.float32)
        return {'X': X, 'H': H}
    _L3_gnn_all = _L3_gnn_setup()
    _L3_gnn_in = {k: v for k, v in _L3_gnn_all.items() if k in ()}
    del _L3_gnn_all
    return {'x': x, 'adj': adj, 'L0_gnn_v_node_feats': _L0_gnn_in['v_node_feats'], 'L0_gnn_uv_W1': _L0_gnn_in['uv_W1'], 'L0_gnn_uv_b1': _L0_gnn_in['uv_b1'], 'L0_gnn_uv_W2': _L0_gnn_in['uv_W2'], 'L0_gnn_uv_b2': _L0_gnn_in['uv_b2'], 'L0_gnn_uv_W3': _L0_gnn_in['uv_W3'], 'L0_gnn_uv_b3': _L0_gnn_in['uv_b3'], 'L0_gnn_vu_W1': _L0_gnn_in['vu_W1'], 'L0_gnn_vu_b1': _L0_gnn_in['vu_b1'], 'L0_gnn_vu_W2': _L0_gnn_in['vu_W2'], 'L0_gnn_vu_b2': _L0_gnn_in['vu_b2'], 'L0_gnn_vu_W3': _L0_gnn_in['vu_W3'], 'L0_gnn_vu_b3': _L0_gnn_in['vu_b3'], 'L1_gnn_W': _L1_gnn_in['W'], 'L1_gnn_b': _L1_gnn_in['b'], 'L2_gnn_W': _L2_gnn_in['W'], 'L2_gnn_b': _L2_gnn_in['b']}

def reference(x, adj, L0_gnn_v_node_feats, L0_gnn_uv_W1, L0_gnn_uv_b1, L0_gnn_uv_W2, L0_gnn_uv_b2, L0_gnn_uv_W3, L0_gnn_uv_b3, L0_gnn_vu_W1, L0_gnn_vu_b1, L0_gnn_vu_W2, L0_gnn_vu_b2, L0_gnn_vu_W3, L0_gnn_vu_b3, L1_gnn_W, L1_gnn_b, L2_gnn_W, L2_gnn_b):
    import jax
    import jax.numpy as jnp

    def _L0_gnn_ref(u_node_feats, v_node_feats, uv_adj_mat, vu_adj_mat, uv_W1, uv_b1, uv_W2, uv_b2, uv_W3, uv_b3, vu_W1, vu_b1, vu_W2, vu_b2, vu_W3, vu_b3):
        import jax, jax.numpy as jnp
        import numpy as np
        NEG_SLOPE = 0.01
        N_U, N_V = (4096, 4096)
        U_F, V_F = (128, 128)
        HIDS = [128, 128]
        NUM_ROUNDS = 3

        def _glorot(key, fan_in, fan_out):
            lim = np.sqrt(6.0 / (fan_in + fan_out)).astype(np.float32)
            return jax.random.uniform(key, (fan_in, fan_out), jnp.float32, -lim, lim)

        def _mlp(x, W1, b1, W2, b2, W3, b3):
            a = jax.nn.leaky_relu
            x = a(x @ W1 + b1, NEG_SLOPE)
            x = a(x @ W2 + b2, NEG_SLOPE)
            return a(x @ W3 + b3, NEG_SLOPE)
        u, v = (u_node_feats, v_node_feats)
        for _ in range(NUM_ROUNDS):
            v = _mlp(uv_adj_mat @ u, uv_W1, uv_b1, uv_W2, uv_b2, uv_W3, uv_b3)
            u = _mlp(vu_adj_mat @ v, vu_W1, vu_b1, vu_W2, vu_b2, vu_W3, vu_b3)
        return v

    def _L1_gnn_ref(X, A, W, b):
        import jax, jax.numpy as jnp
        import numpy as np
        N = 4096
        IN_DIM = 128
        OUT_DIM = 128
        A_hat = A + jnp.eye(A.shape[0], dtype=A.dtype)
        degree = A_hat.sum(axis=1)
        d_inv_sqrt = degree ** (-0.5)
        d_inv_sqrt = jnp.where(jnp.isinf(d_inv_sqrt), 0.0, d_inv_sqrt)
        A_norm = d_inv_sqrt[:, None] * A_hat * d_inv_sqrt[None, :]
        h = A_norm @ X
        return h @ W.T + b

    def _L2_gnn_ref(X, adj, W, b):
        import jax, jax.numpy as jnp
        import numpy as np
        N = 8192
        C = 128
        F = 128
        adj_hat = adj + jnp.eye(adj.shape[0], dtype=adj.dtype)
        d_inv_sqrt = 1.0 / jnp.sqrt(jnp.sum(adj_hat, axis=1))
        adj_norm = adj_hat * d_inv_sqrt[:, None] * d_inv_sqrt[None, :]
        out = adj_norm @ (X @ W) + b
        return jax.nn.relu(out)

    def _L3_gnn_ref(X, H):
        import jax, jax.numpy as jnp
        import numpy as np
        N, E, D = (4096, 4096, 128)
        msg = jnp.matmul(H.T, X)
        inv_deg = 1.0 / H.sum(axis=0)
        inv_deg = jnp.where(jnp.isinf(inv_deg), 0.0, inv_deg)
        return msg * inv_deg[:, None]
    x = _layernorm(x + _L0_gnn_ref(x, L0_gnn_v_node_feats, adj, adj, L0_gnn_uv_W1, L0_gnn_uv_b1, L0_gnn_uv_W2, L0_gnn_uv_b2, L0_gnn_uv_W3, L0_gnn_uv_b3, L0_gnn_vu_W1, L0_gnn_vu_b1, L0_gnn_vu_W2, L0_gnn_vu_b2, L0_gnn_vu_W3, L0_gnn_vu_b3), axis=-1)
    x = _layernorm(x + _L1_gnn_ref(x, adj, L1_gnn_W, L1_gnn_b), axis=-1)
    x = _layernorm(x + _L2_gnn_ref(x, adj, L2_gnn_W, L2_gnn_b), axis=-1)
    x = _layernorm(x + _L3_gnn_ref(x, adj), axis=-1)
    return x

_drawn_inputs = setup_inputs


def setup_inputs(seed=0):
    import zlib

    import numpy as np

    out = dict(_drawn_inputs(seed))
    spreads = {'L0_gnn_uv_b1': (0.0, 0.287),
     'L0_gnn_uv_b2': (0.0, 0.1),
     'L0_gnn_uv_b3': (0.0, 0.1),
     'L0_gnn_vu_b1': (0.0, 0.58),
     'L0_gnn_vu_b2': (0.0, 0.447),
     'L0_gnn_vu_b3': (0.0, 0.322),
     'L1_gnn_b': (0.0, 0.1)}
    factors = {}
    for name, (base, spread) in spreads.items():
        noise = np.random.default_rng([zlib.crc32(name.encode()), seed]).standard_normal(out[name].shape)
        drawn = base * np.exp(spread * noise) if base else spread * noise
        out[name] = jnp.asarray(drawn.astype(out[name].dtype))
    for name, factor in factors.items():
        out[name] = (out[name] * factor).astype(out[name].dtype)
    return out
```

```python
from contextlib import ExitStack
from collections import namedtuple

import concourse.bass as bass
from concourse import mybir

NODES, FEATURES = 4096, 128
P = 128
BLOCK = 512
BLOCKS = NODES // BLOCK
HALF = BLOCKS // 2
TILES = BLOCK // P
NODE_TILES = NODES // P
GRANULE_TILES = 2
GRANULE = GRANULE_TILES * BLOCK
GRANULES_PER_BLOCK = TILES // GRANULE_TILES
RAW_SLOTS = 4
SPLIT_SLOTS = 4
LEAD = 3
ADJ_T = NODES // (TILES * BLOCK)
ADJ = ADJ_T + BLOCKS * BLOCKS
LN_EPS = 1e-5
LEAK = 0.01

MLP_U, MLP_LAST, CONV_1, CONV_2, HYPER = range(5)
KINDS = [MLP_U, MLP_U, MLP_U, MLP_U, MLP_LAST, CONV_1, CONV_2, HYPER]
FIRST_NORMED = BLOCKS * KINDS.index(MLP_LAST)
DEGREE_TURN = FIRST_NORMED

Group = namedtuple("Group", "sweep second first_out step own shared counted adds_partial")
GROUPS = [
    Group(0, 0, 0, +1, (0, 1, 2, 3, 4, 5, 6, 7), (), (), False),
    Group(0, 1, 4, +1, (4, 5, 6, 7), (0, 1, 2, 3), (6, 7), False),
    Group(1, 0, 7, -1, (4, 5, 6, 7), (), (), True),
    Group(1, 1, 3, -1, (0, 1, 2, 3), (7, 6, 5, 4), (4, 5, 6, 7), False),
    Group(2, 0, 0, +1, (3, 2, 1, 0), (), (2, 3), True),
    Group(2, 1, 4, +1, (6, 7, 4, 5), (0, 1, 2, 3), (2, 3, 4, 5), False),
    Group(3, 0, 7, -1, (4, 5, 6, 7), (), (2, 3), True),
    Group(3, 1, 3, -1, (0, 1, 2, 3), (7, 6, 5, 4), (2, 3), False),
    Group(4, 0, 0, +1, (3, 2, 1, 0), (), (), True),
    Group(4, 1, 4, +1, (4, 5, 6, 7), (0, 1, 2, 3), (), False),
    Group(5, 0, 7, -1, (4, 5, 6, 7), (), (), True),
    Group(5, 1, 3, -1, (0, 1, 2, 3), (7, 6, 5, 4), (), False),
    Group(6, 0, 0, +1, (3, 2, 1, 0), (), (), True),
    Group(6, 1, 4, +1, (0, 1, 2, 3, 4, 5, 6, 7), (), (), False),
    Group(7, 0, 7, -1, (0, 1, 2, 3, 4, 5, 6, 7), (), (), False),
    Group(7, 1, 3, -1, (0, 1, 2, 3, 4, 5, 6, 7), (), (), False),
]


def blocks_of(group):
    return group.own + group.shared


def granules_of(group):
    return GRANULES_PER_BLOCK * len(blocks_of(group))


def before(group, count):
    return sum(HALF * count(g) for g in GROUPS[:GROUPS.index(group)])


Turn = namedtuple("Turn", "group i n out tail tail_out kind fresh last granules granule0 block0")


def turn_of(group, i, fresh=False, last=False):
    n = BLOCKS * group.sweep + HALF * group.second + i
    out = group.first_out + group.step * i
    kind = None if fresh and group.sweep == 0 else KINDS[group.sweep - 1 if fresh else group.sweep]
    return Turn(group, i, n, out, n - 1, out if fresh else out - group.step, kind, fresh, last,
                granules_of(group), before(group, granules_of) + i * granules_of(group),
                before(group, lambda g: len(blocks_of(g))) + i * len(blocks_of(group)))


def run_turns(eng, body):
    for group in GROUPS:
        at_end = group is GROUPS[-1]
        if not group.second:
            body(turn_of(group, 0, fresh=True))
        with eng.Fori(0 if group.second else 1, HALF - 1 if at_end else HALF) as i:
            body(turn_of(group, i))
        if at_end:
            body(turn_of(group, HALF - 1, last=True))


def tensor_places(turn):
    if turn.kind == MLP_U:
        return {"dense1": 0, "dense2": 2, "dense3": 4, "natural": 5 if turn.fresh else 6}
    if turn.kind == MLP_LAST:
        start = {"dense1": 0, "dense2": 2, "dense3": 4}
        if turn.fresh:
            return start | {"natural": 5, "turn_x": 5, "project": 5}
        if turn.granules == 8:
            return start | {"natural": 6, "turn_x": 7, "project": 7}
        return start | {"natural": 6, "turn_x": 10, "project": 11}
    if turn.kind == CONV_1:
        return {"natural": 0} | ({"turn_x": 4, "project": 5} if turn.fresh else {"turn_x": 5, "project": 6})
    return {"natural": 0}


def split_places(turn):
    end = turn.granules + LEAD
    if turn.kind == MLP_U:
        return {"leaky1": 5, "leaky2": 7, "leaky3": 9, "operand": 10 if turn.fresh else 11}
    if turn.kind == MLP_LAST:
        start = {"scales": 3, "leaky1": 5, "leaky2": 7, "leaky3": 9}
        if turn.granules == 8:
            at = 10 if turn.fresh else end
            return start | {"moments": at, "root": at, "norm": at, "turned": at, "operand": at}
        return start | {"moments": 11, "root": 11, "norm": 12, "turned": 13, "operand": 14}
    if turn.kind == CONV_1:
        start = {"scales": 3, "moments": 4, "norm": 5, "root": 6}
        return start | ({"turned": 9, "operand": 10} if turn.fresh else {"turned": 10, "operand": 11})
    if turn.kind == CONV_2:
        return {"scales": 3, "moments": 4, "norm": 5, "root": 6, "operand": 8}
    return {"scales": 3, "moments": 4, "norm": 5, "root": 6}


VECTOR_STEPS = {MLP_U: 0, MLP_LAST: 12, CONV_1: 18, CONV_2: 18, HYPER: 15}


def vector_steps_before(kind, tail):
    first = BLOCKS * KINDS.index(kind)
    return sum(BLOCKS * VECTOR_STEPS[k] for k in KINDS[:KINDS.index(kind)]) + (tail - first) * VECTOR_STEPS[kind]


def gnn_stack(nc, stream, weights, mlp_biases, conv_biases, identity, out):
    f32, f32r = mybir.dt.float32, mybir.dt.float32r
    ALU, ACT, AX = mybir.AluOpType, mybir.ActivationFunctionType, mybir.AxisListType
    ds = bass.ds

    ctx = ExitStack()
    with ctx:
        def sb(name, shape, dt=f32):
            return ctx.enter_context(nc.sbuf_tensor(name, shape, dt))

        def bank_pair(name):
            return ctx.enter_context(nc.psum_tensor(name, [P, 2 * BLOCK], f32))

        def bank(name):
            return ctx.enter_context(nc.psum_tensor(name, [P, BLOCK], f32))

        def sem(name):
            return ctx.enter_context(nc.semaphore(name))

        raw = sb("raw", [P, RAW_SLOTS, TILES * BLOCK])
        mat_hi = sb("mat_hi", [P, SPLIT_SLOTS, GRANULE], f32r)
        mat_lo = sb("mat_lo", [P, SPLIT_SLOTS, GRANULE], f32r)
        u_hi = [sb(f"u_hi{k}", [P, NODES], f32r) for k in range(2)]
        u_lo = [sb(f"u_lo{k}", [P, NODES], f32r) for k in range(2)]
        partial = sb("partial", [P, HALF * BLOCK])
        x_res = sb("x_res", [P, NODES])
        row_sums = sb("row_sums", [P, NODES])
        col_sums = sb("col_sums", [P, NODE_TILES, BLOCKS])
        out_t = sb("out_t", [P, BLOCK])
        pre_t = sb("pre_t", [P, BLOCK])
        act_t = sb("act_t", [P, BLOCK])
        sum_n = sb("sum_n", [P, BLOCK])
        conv_n = sb("conv_n", [P, BLOCK])
        normed_n = sb("normed_n", [P, BLOCK])
        normed_t = sb("normed_t", [P, BLOCK])
        stats = sb("stats", [P, TILES, 6])
        moments = sb("moments", [P, TILES, 2])
        wait_carrier = sb("wait_carrier", [P, 1])
        var_eps = sb("var_eps", [P, TILES])
        root = sb("root", [P, TILES])
        inv_root = sb("inv_root", [P, TILES])
        newton = sb("newton", [P, TILES])
        better_root = sb("better_root", [P, TILES])
        rstd = sb("rstd", [P, TILES])
        scale_out = sb("scale_out", [P, TILES])
        scale_in = sb("scale_in", [P, TILES])
        degree = sb("degree", [P, NODE_TILES])
        is_zero = sb("is_zero", [P, NODE_TILES])
        degree_safe = sb("degree_safe", [P, NODE_TILES])
        not_zero = sb("not_zero", [P, NODE_TILES])
        degree_root = sb("degree_root", [P, NODE_TILES])
        degree_inv = sb("degree_inv", [P, NODE_TILES])
        degree_work = sb("degree_work", [P, NODE_TILES])
        degree_better = sb("degree_better", [P, NODE_TILES])
        root_or_zero = sb("root_or_zero", [P, NODE_TILES])
        conv1_scale = sb("conv1_scale", [P, NODE_TILES])
        conv2_scale = sb("conv2_scale", [P, NODE_TILES])
        col_sum = sb("col_sum", [P, NODE_TILES])
        col_zero = sb("col_zero", [P, NODE_TILES])
        col_safe = sb("col_safe", [P, NODE_TILES])
        col_inv = sb("col_inv", [P, NODE_TILES])
        col_not = sb("col_not", [P, NODE_TILES])
        hyper_scale = sb("hyper_scale", [P, NODE_TILES])
        w = sb("w", [P, 8, FEATURES])
        b_mlp = sb("b_mlp", [P, 6])
        b_conv = sb("b_conv", [P, 2, FEATURES])
        ident = sb("ident", [P, P])
        ones = sb("ones", [P, 1])
        pool_scratch = sb("pool_scratch", [P, 1])

        acc = bank_pair("acc")
        part = bank_pair("part")
        dense = [bank("dense0"), bank("dense1")]
        natural = bank("natural")
        projected = bank("projected")

        raw_loaded = [sem(f"raw_loaded{k}") for k in range(RAW_SLOTS)]
        x_loaded = [sem(f"x_loaded{k}") for k in range(BLOCKS)]
        constants_loaded = sem("constants_loaded")
        ones_set = sem("ones_set")
        hi_done = sem("hi_done")
        lo_done = sem("lo_done")
        granule_used = sem("granule_used")
        row_added = sem("row_added")
        evacuated = sem("evacuated")
        part_free = sem("part_free")
        dense_done = [sem(f"dense_done{k}") for k in range(3)]
        pre_ready = [sem(f"pre_ready{k}") for k in range(3)]
        act_ready = [sem(f"act_ready{k}") for k in range(3)]
        natural_done = sem("natural_done")
        u_hi_ready = sem("u_hi_ready")
        u_ready = sem("u_ready")
        scales_ready = sem("scales_ready")
        var_ready = sem("var_ready")
        root_ready = sem("root_ready")
        rstd_ready = sem("rstd_ready")
        normed = sem("normed")
        turned_done = sem("turned_done")
        turned_ready = sem("turned_ready")
        project_done = sem("project_done")
        saved = sem("saved")
        vector_step = sem("vector_step")
        degree_step = sem("degree_step")
        x_hi_ready = sem("x_hi_ready")
        x_split = sem("x_split")
        degree_summed = sem("degree_summed")
        degree_safe_ready = sem("degree_safe_ready")
        degree_root_ready = sem("degree_root_ready")
        degrees_ready = sem("degrees_ready")
        out_stored = sem("out_stored")

        def cols(block):
            return ds(block * BLOCK, BLOCK)

        def tile(t):
            return slice(t * P, (t + 1) * P)

        def bank_of(pair, n):
            return pair[:, ds((n & 1) * BLOCK, BLOCK)]

        def part_turn(turn):
            return before(turn.group, lambda g: 1 if g.shared else 0) + turn.i

        def partial_cols(turn):
            low = HALF if max(turn.group.first_out, turn.group.first_out + turn.group.step) >= HALF else 0
            return cols(turn.out - low)

        def is_counted(turn, k):
            return k < turn.granules and k // GRANULES_PER_BLOCK in turn.group.counted

        block = ctx.enter_context(nc.Block())

        @block.sync
        def _(sp):
            def turn_loads(turn):
                first = ADJ if turn.group.sweep == len(KINDS) - 1 else ADJ_T
                for place, jb in enumerate(blocks_of(turn.group)):
                    number = turn.block0 + place
                    slot = place % RAW_SLOTS
                    if not (isinstance(number, int) and number < RAW_SLOTS):
                        sp.wait_ge(lo_done, GRANULES_PER_BLOCK * (number - RAW_SLOTS + 1))
                    sp.dma_start(raw[:, slot, :],
                                 stream[ds(turn.out * BLOCKS + (first + jb), 1), :, :].rearrange("o p n -> (o p) n"))\
                      .then_inc(raw_loaded[slot], 16)

            run_turns(sp, turn_loads)

        @block.gpsimd
        def _(pool):
            nc.gpsimd.memset(ones[:], 1.0).then_inc(ones_set, 1)
            pool.wait_ge(ones_set, 1)
            nc.gpsimd.memset(row_sums[:], 0.0).then_inc(row_added, 1)
            nc.gpsimd.memset(normed_n[:, 0:1], 0.0).then_inc(saved, 1)
            for sweep in range(KINDS.index(MLP_LAST), len(KINDS)):
                group = GROUPS[2 * sweep]
                with pool.Fori(0, BLOCKS) as i:
                    tail = BLOCKS * sweep - FIRST_NORMED + i
                    out_block = group.first_out + group.step * i
                    pool.wait_ge(normed, tail + 1)
                    if KINDS[sweep] != HYPER:
                        nc.gpsimd.tensor_copy(x_res[:, cols(out_block)], normed_n[:]).then_inc(saved, 1)
                    else:
                        pool.dma_start(out[ds(out_block, 1), :, :].rearrange("o p n -> (o p) n"),
                                       normed_n[:]).then_inc(out_stored, 16)
                        pool.wait_ge(out_stored, 16 * (i + 1))
                        nc.gpsimd.tensor_tensor(pool_scratch[:], ones[:], ones[:], ALU.add).then_inc(saved, 1)
            pool.wait_ge(out_stored, 16 * BLOCKS)

        @block.scalar
        def _(act):
            for c in range(BLOCKS):
                act.dma_start(x_res[:, c * BLOCK:(c + 1) * BLOCK],
                              stream[c // TILES, :, (c % TILES) * BLOCK:(c % TILES + 1) * BLOCK])\
                   .then_inc(x_loaded[c], 16)
            act.dma_start(w[:], weights).then_inc(constants_loaded, 16)
            act.dma_start(b_mlp[:], mlp_biases).then_inc(constants_loaded, 16)
            act.dma_start(ident[:], identity).then_inc(constants_loaded, 16)
            for k in range(2):
                act.dma_start(b_conv[:, k, :], conv_biases[k, :].partition_broadcast(P))\
                   .then_inc(constants_loaded, 16)

            def granule(turn, k):
                number = turn.granule0 + k
                block_place = k // GRANULES_PER_BLOCK
                slot = block_place % RAW_SLOTS
                if k % GRANULES_PER_BLOCK == 0:
                    act.wait_ge(raw_loaded[slot], 16 * (turn_block_round(turn) + block_place // RAW_SLOTS + 1))
                if not (isinstance(number, int) and number < SPLIT_SLOTS):
                    act.wait_ge(granule_used, number - SPLIT_SLOTS + 1)
                start = (k % GRANULES_PER_BLOCK) * GRANULE
                if not is_counted(turn, k):
                    nc.scalar.activation(mat_hi[:, k % SPLIT_SLOTS, :], raw[:, slot, start:start + GRANULE],
                                         ACT.Copy).then_inc(hi_done, 1)
                    return
                for t in range(GRANULE_TILES):
                    jt = blocks_of(turn.group)[block_place] * TILES + (k % GRANULES_PER_BLOCK) * GRANULE_TILES + t
                    done = nc.scalar.activation(
                        mat_hi[:, k % SPLIT_SLOTS, t * BLOCK:(t + 1) * BLOCK],
                        raw[:, slot, start + t * BLOCK:start + (t + 1) * BLOCK], ACT.Copy,
                        accum_out=col_sums[:, jt, ds(turn.out, 1)])
                done.then_inc(hi_done, 1)

            def turn_block_round(turn):
                g = turn.group
                return before(g, lambda q: len(blocks_of(q))) // RAW_SLOTS + turn.i * (len(blocks_of(g)) // RAW_SLOTS)

            def tail_step(turn, step):
                e, kind = turn.tail, turn.kind
                norm_tail = e - FIRST_NORMED
                sweep = turn.group.sweep - (1 if turn.fresh else 0)
                if step in ("leaky1", "leaky2", "leaky3"):
                    k = int(step[-1]) - 1
                    bias = (sweep % 2) * 3 + k
                    act.wait_ge(dense_done[k], e + 1)
                    nc.scalar.activation(pre_t[:], dense[k % 2][:], ACT.Identity,
                                         bias=b_mlp[:, bias:bias + 1]).then_inc(pre_ready[k], 1)
                elif step == "scales":
                    if kind == MLP_LAST:
                        act.wait_ge(degrees_ready, 1)
                    if kind == HYPER:
                        act.wait_ge(normed, norm_tail)
                    else:
                        act.wait_ge(u_ready, e + 1)
                    made = None
                    if kind in (CONV_1, CONV_2, HYPER):
                        table = {CONV_1: conv1_scale, CONV_2: conv2_scale, HYPER: hyper_scale}[kind]
                        made = nc.scalar.activation(scale_out[:], table[:, ds(turn.tail_out * TILES, TILES)], ACT.Copy)
                    if kind in (MLP_LAST, CONV_1):
                        table = {MLP_LAST: conv1_scale, CONV_1: conv2_scale}[kind]
                        made = nc.scalar.activation(scale_in[:], table[:, ds(turn.tail_out * TILES, TILES)], ACT.Copy)
                    made.then_inc(scales_ready, 1)
                elif step == "root":
                    act.wait_ge(var_ready, norm_tail + 1)
                    nc.scalar.activation(root[:], var_eps[:], ACT.Sqrt).then_inc(root_ready, 1)
                elif step == "turned":
                    act.wait_ge(turned_done, norm_tail + 1)
                    nc.scalar.activation(normed_t[:], dense[1][:], ACT.Copy).then_inc(turned_ready, 1)
                elif step == "operand":
                    target = u_hi[(sweep + 1) % 2]
                    if kind == MLP_U:
                        act.wait_ge(natural_done, e + 1)
                        done = nc.scalar.activation(target[:, cols(turn.tail_out)], natural[:], ACT.Copy)
                    elif kind == CONV_2:
                        act.wait_ge(normed, norm_tail + 1)
                        done = nc.scalar.activation(target[:, cols(turn.tail_out)], normed_n[:], ACT.Copy)
                    else:
                        act.wait_ge(project_done, norm_tail + 1)
                        act.wait_ge(scales_ready, norm_tail + 1)
                        for c in range(TILES):
                            done = nc.scalar.activation(
                                target[:, ds(turn.tail_out * BLOCK + c * P, P)], projected[:, tile(c)],
                                ACT.Copy, scale=scale_in[:, c:c + 1])
                    done.then_inc(u_hi_ready, 1)

            def split_turn(turn):
                places = split_places(turn) if turn.kind is not None else {}
                order = ("scales", "leaky1", "leaky2", "leaky3", "root", "turned", "operand")
                for k in range(LEAD, turn.granules + LEAD + 1):
                    for step in order:
                        if places.get(step) == k:
                            tail_step(turn, step)
                    if k < turn.granules + (0 if turn.last else LEAD):
                        granule(turn, k)
                if turn.group.shared:
                    act.wait_ge(granule_used, turn.granule0 + turn.granules)
                    nc.scalar.activation(partial[:, partial_cols(turn)], bank_of(part, turn.n),
                                         ACT.Copy).then_inc(part_free, 1)
                if isinstance(turn.n, int) and turn.n == DEGREE_TURN:
                    act.wait_ge(degree_safe_ready, 1)
                    nc.scalar.activation(degree_root[:], degree_safe[:], ACT.Sqrt).then_inc(degree_root_ready, 1)

            first = turn_of(GROUPS[0], 0, fresh=True)

            def split_x(c):
                act.wait_ge(x_loaded[c], 16)
                done = nc.scalar.activation(u_hi[0][:, c * BLOCK:(c + 1) * BLOCK],
                                            x_res[:, c * BLOCK:(c + 1) * BLOCK], ACT.Copy)
                done.then_inc(x_hi_ready, 1)

            split_x(0)
            for k in range(LEAD):
                granule(first, k)
                split_x(k + 1)
            for c in range(LEAD + 1, BLOCKS):
                split_x(c)
            act.wait_ge(constants_loaded, 16 * 5)
            nc.scalar.activation(root[:], b_mlp[:, 0:TILES], ACT.Copy).then_inc(part_free, 2)
            run_turns(act, split_turn)
            finale = turn_of(GROUPS[-1], HALF)
            for step in ("scales", "root"):
                tail_step(finale, step)

        @block.vector
        def _(dve):
            def granule(turn, k):
                number = turn.granule0 + k
                slot = (k // GRANULES_PER_BLOCK) % RAW_SLOTS
                start = (k % GRANULES_PER_BLOCK) * GRANULE
                dve.wait_ge(hi_done, number + 1)
                if is_counted(turn, k):
                    g = turn.group
                    adds_before = (before(g, lambda q: len(q.counted) * TILES)
                                   + turn.i * len(g.counted) * TILES
                                   + sorted(g.counted).index(k // GRANULES_PER_BLOCK) * TILES
                                   + (k % GRANULES_PER_BLOCK) * GRANULE_TILES)
                    for t in range(GRANULE_TILES):
                        dve.wait_ge(row_added, adds_before + t + 1)
                        nc.vector.tensor_tensor(row_sums[:, cols(turn.out)], row_sums[:, cols(turn.out)],
                                                raw[:, slot, start + t * BLOCK:start + (t + 1) * BLOCK],
                                                ALU.add).then_inc(row_added, 1)
                nc.vector.tensor_tensor(mat_lo[:, k % SPLIT_SLOTS, :], raw[:, slot, start:start + GRANULE],
                                        mat_hi[:, k % SPLIT_SLOTS, :].bitcast(f32),
                                        ALU.subtract).then_inc(lo_done, 1)

            def tail_step(turn, step, count):
                e, kind, where = turn.tail, turn.kind, turn.tail_out
                norm_tail = e - FIRST_NORMED
                sweep = turn.group.sweep - (1 if turn.fresh else 0)
                here, there = sweep % 2, (sweep + 1) % 2

                def signalled(instruction):
                    count[0] += 1
                    instruction.then_inc(vector_step, 1)

                def wait_own():
                    dve.wait_ge(vector_step, vector_steps_before(kind, e) + count[0])

                if step in ("leaky1", "leaky2", "leaky3"):
                    k = int(step[-1]) - 1
                    dve.wait_ge(pre_ready[k], e + 1)
                    nc.vector.scalar_tensor_tensor(act_t[:], pre_t[:], LEAK, pre_t[:], ALU.mult,
                                                   ALU.max).then_inc(act_ready[k], 1)
                elif step == "moments":
                    dve.wait_ge(natural_done, e + 1)
                    x_here = x_res[:, cols(where)]
                    if kind != MLP_LAST:
                        dve.wait_ge(saved, norm_tail + 1)
                    if kind == MLP_LAST:
                        signalled(nc.vector.tensor_tensor(sum_n[:], natural[:], x_here, ALU.add))
                    elif kind in (CONV_1, CONV_2):
                        signalled(nc.vector.tensor_tensor(sum_n[:], natural[:],
                                                          u_hi[here][:, cols(where)].bitcast(f32), ALU.add))
                        wait_own()
                        signalled(nc.vector.tensor_tensor(conv_n[:], sum_n[:],
                                                          u_lo[here][:, cols(where)].bitcast(f32), ALU.add))
                        wait_own()
                        dve.wait_ge(scales_ready, norm_tail + 1)
                        for c in range(TILES):
                            signalled(nc.vector.scalar_tensor_tensor(
                                sum_n[:, tile(c)], conv_n[:, tile(c)], scale_out[:, c:c + 1],
                                b_conv[:, kind - CONV_1, :], ALU.mult, ALU.add))
                        wait_own()
                        if kind == CONV_1:
                            signalled(nc.vector.tensor_tensor(conv_n[:], sum_n[:], x_here, ALU.add))
                        else:
                            signalled(nc.vector.scalar_tensor_tensor(conv_n[:], sum_n[:], 0.0, x_here,
                                                                     ALU.max, ALU.add))
                    else:
                        dve.wait_ge(scales_ready, norm_tail + 1)
                        for c in range(TILES):
                            signalled(nc.vector.scalar_tensor_tensor(
                                sum_n[:, tile(c)], natural[:, tile(c)], scale_out[:, c:c + 1],
                                x_res[:, ds(where * BLOCK + c * P, P)], ALU.mult, ALU.add))
                    summed = conv_n if kind in (CONV_1, CONV_2) else sum_n
                    wait_own()
                    for c in range(TILES):
                        signalled(nc.vector.bn_stats(stats[:, c, :], summed[:, tile(c)]))
                    wait_own()
                    nc.vector.memset(wait_carrier[:], 0.0)
                    for c in range(TILES):
                        signalled(nc.vector.bn_aggr(moments[:, c, :], stats[:, c, :]))
                    wait_own()
                    nc.vector.tensor_scalar(var_eps[:], moments[:, :, 1], LN_EPS, None,
                                            ALU.add).then_inc(var_ready, 1)
                elif step == "norm":
                    dve.wait_ge(root_ready, norm_tail + 1)
                    signalled(nc.vector.reciprocal(inv_root[:], root[:]))
                    wait_own()
                    signalled(nc.vector.scalar_tensor_tensor(newton[:], var_eps[:], 0.5, inv_root[:],
                                                             ALU.mult, ALU.mult))
                    wait_own()
                    signalled(nc.vector.scalar_tensor_tensor(better_root[:], root[:], 0.5, newton[:],
                                                             ALU.mult, ALU.add))
                    wait_own()
                    dve.wait_ge(saved, norm_tail + 1)
                    rstd_made = nc.vector.reciprocal(rstd[:], better_root[:])
                    rstd_made.then_inc(rstd_ready, 1)
                    dve.wait_ge(rstd_ready, norm_tail + 1)
                    summed = conv_n if kind in (CONV_1, CONV_2) else sum_n
                    for c in range(TILES):
                        done = nc.vector.tensor_scalar(normed_n[:, tile(c)], summed[:, tile(c)],
                                                       moments[:, c, 0:1], rstd[:, c:c + 1],
                                                       ALU.subtract, ALU.mult)
                    done.then_inc(normed, 1)
                    assert count[0] == VECTOR_STEPS[kind], (kind, count[0])
                elif step == "operand":
                    dve.wait_ge(u_hi_ready, e + 1)
                    high, low = u_hi[there], u_lo[there]
                    if kind in (MLP_U, CONV_2):
                        source = natural if kind == MLP_U else normed_n
                        done = nc.vector.tensor_tensor(low[:, cols(where)], source[:],
                                                       high[:, cols(where)].bitcast(f32), ALU.subtract)
                    else:
                        for c in range(TILES):
                            here_c = ds(where * BLOCK + c * P, P)
                            done = nc.vector.scalar_tensor_tensor(
                                low[:, here_c], projected[:, tile(c)], scale_in[:, c:c + 1],
                                high[:, here_c].bitcast(f32), ALU.mult, ALU.subtract)
                    done.then_inc(u_ready, 1)

            def degrees():
                steps = [0]

                def chained(instruction):
                    steps[0] += 1
                    instruction.then_inc(degree_step, 1)
                    dve.wait_ge(degree_step, steps[0])

                dve.wait_ge(degree_summed, 1)
                chained(nc.vector.tensor_scalar(degree[:], projected[:, 0:NODE_TILES], 1.0, None, ALU.add))
                chained(nc.vector.tensor_scalar(is_zero[:], degree[:], 0.0, None, ALU.is_equal))
                nc.vector.tensor_tensor(degree_safe[:], degree[:], is_zero[:], ALU.add)\
                  .then_inc(degree_safe_ready, 1)
                chained(nc.vector.tensor_scalar(not_zero[:], is_zero[:], -1.0, 1.0, ALU.mult, ALU.add))
                chained(nc.vector.tensor_reduce(col_sum[:], col_sums[:], AX.X, ALU.add))
                chained(nc.vector.tensor_scalar(col_zero[:], col_sum[:], 0.0, None, ALU.is_equal))
                chained(nc.vector.tensor_tensor(col_safe[:], col_sum[:], col_zero[:], ALU.add))
                chained(nc.vector.tensor_scalar(col_not[:], col_zero[:], -1.0, 1.0, ALU.mult, ALU.add))
                chained(nc.vector.reciprocal(col_inv[:], col_safe[:]))
                chained(nc.vector.tensor_tensor(hyper_scale[:], col_inv[:], col_not[:], ALU.mult))
                dve.wait_ge(degree_root_ready, 1)
                chained(nc.vector.reciprocal(degree_inv[:], degree_root[:]))
                chained(nc.vector.scalar_tensor_tensor(degree_work[:], degree_safe[:], 0.5, degree_inv[:],
                                                       ALU.mult, ALU.mult))
                chained(nc.vector.scalar_tensor_tensor(degree_better[:], degree_root[:], 0.5, degree_work[:],
                                                       ALU.mult, ALU.add))
                chained(nc.vector.tensor_tensor(root_or_zero[:], degree_better[:], not_zero[:], ALU.mult))
                chained(nc.vector.reciprocal(conv2_scale[:], root_or_zero[:]))
                chained(nc.vector.reciprocal(degree_inv[:], degree_better[:]))
                nc.vector.tensor_tensor(conv1_scale[:], degree_inv[:], not_zero[:], ALU.mult)\
                  .then_inc(degrees_ready, 1)

            def split_turn(turn):
                places = split_places(turn) if turn.kind is not None else {}
                count = [0]
                for k in range(LEAD, turn.granules + LEAD + 1):
                    for step in ("leaky1", "leaky2", "leaky3", "moments", "norm", "operand"):
                        if places.get(step) == k:
                            tail_step(turn, step, count)
                    if k < turn.granules + (0 if turn.last else LEAD):
                        granule(turn, k)
                dve.wait_ge(granule_used, turn.granule0 + turn.granules)
                if turn.group.adds_partial:
                    nc.vector.tensor_tensor(out_t[:], bank_of(acc, turn.n), partial[:, partial_cols(turn)],
                                            ALU.add).then_inc(evacuated, 1)
                else:
                    nc.vector.tensor_copy(out_t[:], bank_of(acc, turn.n)).then_inc(evacuated, 1)
                if isinstance(turn.n, int) and turn.n == DEGREE_TURN:
                    degrees()

            first = turn_of(GROUPS[0], 0, fresh=True)

            def split_x(c):
                dve.wait_ge(x_hi_ready, c + 1)
                here = slice(c * BLOCK, (c + 1) * BLOCK)
                nc.vector.tensor_tensor(u_lo[0][:, here], x_res[:, here], u_hi[0][:, here].bitcast(f32),
                                        ALU.subtract).then_inc(x_split, 1)
                if c == BLOCKS - 1:
                    dve.wait_ge(x_split, BLOCKS)
                    nc.vector.memset(inv_root[:], 0.0).then_inc(u_ready, 1)

            split_x(0)
            for k in range(LEAD):
                granule(first, k)
                split_x(k + 1)
            for c in range(LEAD + 1, BLOCKS):
                split_x(c)
            nc.vector.memset(newton[:], 0.0).then_inc(evacuated, 1)
            run_turns(dve, split_turn)
            finale = turn_of(GROUPS[-1], HALF)
            count = [0]
            for step in ("moments", "norm"):
                tail_step(finale, step, count)

        @block.tensor
        def _(pe):
            def tail_step(turn, step):
                e, kind = turn.tail, turn.kind
                norm_tail = e - FIRST_NORMED
                sweep = turn.group.sweep - (1 if turn.fresh else 0)
                if step in ("dense1", "dense2", "dense3"):
                    k = int(step[-1]) - 1
                    if k == 0:
                        pe.wait_ge(evacuated, e + 2)
                    else:
                        pe.wait_ge(act_ready[k - 1], e + 1)
                    nc.tensor.matmul(dense[k % 2][:], w[:, (sweep % 2) * 3 + k, :], (act_t if k else out_t)[:],
                                     start=True, stop=True).then_inc(dense_done[k], 1)
                elif step == "natural":
                    if kind in (MLP_U, MLP_LAST):
                        pe.wait_ge(act_ready[2], e + 1)
                    else:
                        pe.wait_ge(evacuated, e + 2)
                    if kind == HYPER:
                        pe.wait_ge(normed, norm_tail)
                    else:
                        pe.wait_ge(u_ready, e + 1)
                    source = act_t if kind in (MLP_U, MLP_LAST) else out_t
                    for c in range(TILES):
                        done = nc.tensor.transpose(natural[:, tile(c)], source[:, tile(c)], ident[:])
                    done.then_inc(natural_done, 1)
                elif step == "turn_x":
                    pe.wait_ge(normed, norm_tail + 1)
                    for c in range(TILES):
                        done = nc.tensor.transpose(dense[1][:, tile(c)], normed_n[:, tile(c)], ident[:])
                    done.then_inc(turned_done, 1)
                elif step == "project":
                    pe.wait_ge(turned_ready, norm_tail + 1)
                    if kind == MLP_LAST:
                        pe.wait_ge(degrees_ready, 1)
                    for c in range(TILES):
                        done = nc.tensor.matmul(projected[:, tile(c)], normed_t[:, tile(c)],
                                                w[:, 6 if kind == MLP_LAST else 7, :], start=True, stop=True)
                    done.then_inc(project_done, 1)

            def sum_degrees():
                counted = sum(HALF * TILES * len(g.counted) for g in GROUPS)
                assert counted == BLOCKS * NODE_TILES
                pe.wait_ge(row_added, counted + 1)
                pe.wait_ge(ones_set, 1)
                for t in range(NODE_TILES):
                    done = nc.tensor.matmul(projected[:, t:t + 1], row_sums[:, tile(t)], ones[:],
                                            start=True, stop=True)
                done.then_inc(degree_summed, 1)

            def products(turn):
                group, n = turn.group, turn.n
                places = tensor_places(turn) if turn.kind is not None else {}
                here, there = group.sweep % 2, (group.sweep + 1) % 2
                if not (isinstance(n, int) and n == 0):
                    pe.wait_ge(evacuated, n)
                    if turn.fresh:
                        pe.wait_ge(u_ready, n)
                if group.shared:
                    pe.wait_ge(part_free, part_turn(turn) + 1)
                acc_out, part_out = bank_of(acc, n), bank_of(part, n)
                last_own, last_shared = len(group.own) - 1, len(blocks_of(group)) - 1
                for k in range(turn.granules):
                    place = k // GRANULES_PER_BLOCK
                    jb, shared = blocks_of(group)[place], place > last_own
                    if k % GRANULES_PER_BLOCK == 0:
                        if isinstance(n, int) and n == 0:
                            pe.wait_ge(x_split, place + 1)
                        elif (turn.fresh and place == last_own) or (group.shared and place == last_shared):
                            pe.wait_ge(u_ready, n + 1)
                    pe.wait_ge(lo_done, turn.granule0 + k + 1)
                    for target, parity in ((acc_out, here), (part_out, there))[:1 + shared]:
                        first_place = len(group.own) if target is part_out else 0
                        for t in range(GRANULE_TILES):
                            jt = jb * TILES + (k % GRANULES_PER_BLOCK) * GRANULE_TILES + t
                            start = place == first_place and k % GRANULES_PER_BLOCK == 0 and t == 0
                            stop = k == turn.granules - 1 and t == GRANULE_TILES - 1
                            strip = slice(t * BLOCK, (t + 1) * BLOCK)
                            hi, lo = mat_hi[:, k % SPLIT_SLOTS, strip], mat_lo[:, k % SPLIT_SLOTS, strip]
                            nc.tensor.matmul(target, u_hi[parity][:, tile(jt)], hi, start=start, stop=False)
                            nc.tensor.matmul(target, u_hi[parity][:, tile(jt)], lo, start=False, stop=False)
                            done = nc.tensor.matmul(target, u_lo[parity][:, tile(jt)], hi,
                                                    start=False, stop=stop)
                    done.then_inc(granule_used, 1)
                    for step in ("dense1", "dense2", "dense3", "natural", "turn_x", "project"):
                        if places.get(step) == k:
                            tail_step(turn, step)
                    if k == LEAD and isinstance(n, int) and n == DEGREE_TURN:
                        sum_degrees()

            pe.wait_ge(constants_loaded, 16 * 5)
            run_turns(pe, products)
            tail_step(turn_of(GROUPS[-1], HALF), "natural")


def kernel(x, adj, L0_gnn_v_node_feats, L0_gnn_uv_W1, L0_gnn_uv_b1, L0_gnn_uv_W2, L0_gnn_uv_b2,
           L0_gnn_uv_W3, L0_gnn_uv_b3, L0_gnn_vu_W1, L0_gnn_vu_b1, L0_gnn_vu_W2, L0_gnn_vu_b2,
           L0_gnn_vu_W3, L0_gnn_vu_b3, L1_gnn_W, L1_gnn_b, L2_gnn_W, L2_gnn_b):
    import numpy as np
    import concourse.bacc as bacc
    from concourse.bass_utils import run_bass_kernel_spmd

    a, x = np.asarray(adj), np.asarray(x)
    strip = (-1, P, TILES * BLOCK)
    arrays = {
        "stream": np.concatenate([
            x.reshape(ADJ_T, -1, P, FEATURES).transpose(0, 2, 1, 3).reshape(strip),
            a.reshape(BLOCKS, BLOCK, BLOCKS, TILES, P).transpose(0, 2, 4, 3, 1).reshape(strip),
            a.reshape(BLOCKS, TILES, P, BLOCKS, BLOCK).transpose(3, 0, 2, 1, 4).reshape(strip)]),
        "weights": np.stack([np.asarray(m) for m in (
            L0_gnn_uv_W1, L0_gnn_uv_W2, L0_gnn_uv_W3, L0_gnn_vu_W1, L0_gnn_vu_W2, L0_gnn_vu_W3,
            np.asarray(L1_gnn_W).T, L2_gnn_W)], axis=1),
        "mlp_biases": np.stack([np.asarray(b) for b in (
            L0_gnn_uv_b1, L0_gnn_uv_b2, L0_gnn_uv_b3, L0_gnn_vu_b1, L0_gnn_vu_b2, L0_gnn_vu_b3)], axis=1),
        "conv_biases": np.stack([np.asarray(L1_gnn_b), np.asarray(L2_gnn_b)]),
        "identity": np.eye(P, dtype=np.float32),
    }
    arrays = {name: np.ascontiguousarray(value) for name, value in arrays.items()}
    nc = bacc.Bacc("TRN2", target_bir_lowering=False, num_devices=1)
    args = [nc.dram_tensor(name, v.shape, mybir.dt.from_np(v.dtype), kind="ExternalInput").ap()
            for name, v in arrays.items()]
    out = nc.dram_tensor("out_blocks", (BLOCKS, P, BLOCK), mybir.dt.float32, kind="ExternalOutput").ap()
    gnn_stack(nc, *args, out)
    got = run_bass_kernel_spmd(nc, [arrays], core_ids=[0]).results[0]["out_blocks"]
    return got.reshape(BLOCKS, P, TILES, FEATURES).transpose(0, 2, 1, 3).reshape(NODES, FEATURES)
```

```python
from contextlib import ExitStack
from collections import namedtuple

import concourse.bass as bass
from concourse import mybir

NODES, FEATURES = 4096, 128
P = 128
BLOCK = 512
BLOCKS = NODES // BLOCK
HALF = BLOCKS // 2
TILES = BLOCK // P
NODE_TILES = NODES // P
GRANULE_TILES = 2
GRANULE = GRANULE_TILES * BLOCK
GRANULES_PER_BLOCK = TILES // GRANULE_TILES
RAW_SLOTS = 4
SPLIT_SLOTS = 4
LEAD = 3
ADJ_T = NODES // (TILES * BLOCK)
ADJ = ADJ_T + BLOCKS * BLOCKS
LN_EPS = 1e-5
LEAK = 0.01

MLP_U, MLP_LAST, CONV_1, CONV_2, HYPER = range(5)
KINDS = [MLP_U, MLP_U, MLP_U, MLP_U, MLP_LAST, CONV_1, CONV_2, HYPER]
FIRST_NORMED = BLOCKS * KINDS.index(MLP_LAST)
FIRST_SCALED = BLOCKS * KINDS.index(CONV_1)
DEGREE_TURN = FIRST_NORMED

Group = namedtuple("Group", "sweep second first_out step own shared counted adds_partial")
GROUPS = [
    Group(0, 0, 0, +1, (0, 1, 2, 3, 4, 5, 6, 7), (), (), False),
    Group(0, 1, 4, +1, (4, 5, 6, 7), (0, 1, 2, 3), (2, 3, 6, 7), False),
    Group(1, 0, 7, -1, (4, 5, 6, 7), (), (), True),
    Group(1, 1, 3, -1, (0, 1, 2, 3), (7, 6, 5, 4), (2, 3, 4, 5), False),
    Group(2, 0, 0, +1, (3, 2, 1, 0), (), (), True),
    Group(2, 1, 4, +1, (5, 4, 6, 7), (1, 0, 2, 3), (2, 3, 4, 5), False),
    Group(3, 0, 7, -1, (4, 5, 6, 7), (), (), True),
    Group(3, 1, 3, -1, (1, 0, 2, 3), (6, 7, 5, 4), (2, 3, 6, 7), False),
    Group(4, 0, 0, +1, (3, 2, 1, 0), (), (), True),
    Group(4, 1, 4, +1, (4, 5, 6, 7), (0, 1, 2, 3), (), False),
    Group(5, 0, 7, -1, (4, 5, 6, 7), (), (), True),
    Group(5, 1, 3, -1, (0, 1, 2, 3), (7, 6, 5, 4), (), False),
    Group(6, 0, 0, +1, (3, 2, 1, 0), (), (), True),
    Group(6, 1, 4, +1, (0, 1, 2, 3, 4, 5, 6, 7), (), (), False),
    Group(7, 0, 7, -1, (0, 1, 2, 3, 4, 5, 6, 7), (), (), False),
    Group(7, 1, 3, -1, (0, 1, 2, 3, 4, 5, 6, 7), (), (), False),
]


def blocks_of(group):
    if not group.shared:
        return group.own
    return tuple(b for pair in zip(group.own, group.shared) for b in pair)


def granules_of(group):
    return GRANULES_PER_BLOCK * len(blocks_of(group))


def before(group, count):
    return sum(HALF * count(g) for g in GROUPS[:GROUPS.index(group)])


Turn = namedtuple("Turn", "group i n out tails fresh last granules granule0 block0")
Tail = namedtuple("Tail", "kind n out sweep stage")
ALL, FIRST, SECOND = range(3)
LONG_TAILS = (MLP_LAST, CONV_1)


def turn_of(group, i, last=False):
    sweep, per_turn = group.sweep, granules_of(group)
    fresh = isinstance(i, int) and i == 0 and not group.second
    first_of_group = isinstance(i, int) and i == 0
    n = BLOCKS * sweep + HALF * group.second + i
    out = group.first_out + group.step * i
    tails = []
    if fresh:
        if sweep:
            tails.append(Tail(KINDS[sweep - 1], n - 1, out, sweep - 1, ALL))
    else:
        kind = KINDS[sweep]
        split = kind in LONG_TAILS
        second_turn = isinstance(i, int) and i == 1 and not group.second
        if split and not second_turn and (not group.second or first_of_group):
            tails.append(Tail(kind, n - 2, out - 2 * group.step, sweep, SECOND))
        tails.append(Tail(kind, n - 1, out - group.step, sweep, FIRST if split and not group.second else ALL))
    return Turn(group, i, n, out, tails, fresh, last, per_turn,
                before(group, granules_of) + i * per_turn,
                before(group, lambda g: len(blocks_of(g))) + i * len(blocks_of(group)))


def run_turns(eng, body):
    for group in GROUPS:
        split = KINDS[group.sweep] in LONG_TAILS
        at_end = group is GROUPS[-1]
        start = (int(split) if group.second else 1 + split)
        for i in range(start):
            body(turn_of(group, i))
        with eng.Fori(start, HALF - 1 if at_end else HALF) as i:
            body(turn_of(group, i))
        if at_end:
            body(turn_of(group, HALF - 1, last=True))


def tensor_places(turn, tail):
    if tail.kind == MLP_U:
        return {"dense1": 0, "dense2": 2, "dense3": 4, "natural": 5 if turn.fresh else 6}
    if tail.kind == MLP_LAST:
        start = {"dense1": 0, "dense2": 2, "dense3": 4}
        if tail.stage == SECOND:
            return {"turn_x": 5, "project": 6}
        if tail.stage == FIRST:
            return start | {"natural": 7}
        if turn.fresh:
            return start | {"natural": 5, "turn_x": 5, "project": 5}
        return start | {"natural": 7, "turn_x": 9, "project": 11}
    if tail.kind == CONV_1:
        if tail.stage == SECOND:
            return {"turn_x": 0, "project": 2}
        if tail.stage == FIRST:
            return {"natural": 1}
        return {"natural": 1} | ({"turn_x": 4, "project": 5} if turn.fresh else {"turn_x": 5, "project": 7})
    return {"natural": 0}


def split_places(turn, tail):
    if tail.kind == MLP_U:
        return {"leaky1": 5, "leaky2": 7, "leaky3": 9, "operand": 10 if turn.fresh else 11}
    if tail.kind == MLP_LAST:
        start = {"leaky1": 4, "leaky2": 7, "leaky3": 9}
        if tail.stage == SECOND:
            return {"scale_in": 4, "moments": 4, "root": 6, "norm": 6, "turned": 10, "operand": 11}
        if tail.stage == FIRST:
            return start
        if turn.fresh:
            return start | {"scale_in": 4, "moments": 10, "root": 10, "norm": 10, "turned": 10, "operand": 10}
        return start | {"scale_in": 11, "moments": 10, "root": 11, "norm": 11, "turned": 13, "operand": 15}
    if tail.kind == CONV_1:
        if tail.stage == SECOND:
            return {"scale_in": 3, "turned": 4, "operand": 6}
        if tail.stage == FIRST:
            return {"scale_out": 3, "moments": 5, "root": 7, "norm": 8}
        if turn.fresh:
            return {"scale_out": 3, "scale_in": 3, "moments": 4, "root": 6, "norm": 5, "turned": 9, "operand": 10}
        return {"scale_out": 3, "moments": 5, "root": 7, "norm": 7, "scale_in": 7, "turned": 10, "operand": 11}
    if tail.kind == CONV_2:
        return {"scale_out": 3, "moments": 4, "root": 6, "norm": 6, "operand": 8}
    return {"scale_out": 3, "moments": 4, "root": 6, "norm": 6}


def steps_at(turn, places, order, k):
    return [(tail, step) for tail in turn.tails for step in order if places(turn, tail).get(step) == k]


VECTOR_STEPS = {MLP_U: 0, MLP_LAST: 12, CONV_1: 16, CONV_2: 17, HYPER: 15}


def vector_steps_before(tail):
    kinds = KINDS[:tail.sweep]
    return sum(BLOCKS * VECTOR_STEPS[k] for k in kinds) + (tail.n - BLOCKS * tail.sweep) * VECTOR_STEPS[tail.kind]


def gnn_stack(nc, stream, weights, mlp_biases, conv_biases, identity, out):
    f32, f32r = mybir.dt.float32, mybir.dt.float32r
    ALU, ACT, AX = mybir.AluOpType, mybir.ActivationFunctionType, mybir.AxisListType
    ds = bass.ds

    ctx = ExitStack()
    with ctx:
        def sb(name, shape, dt=f32):
            return ctx.enter_context(nc.sbuf_tensor(name, shape, dt))

        def bank_pair(name):
            return ctx.enter_context(nc.psum_tensor(name, [P, 2 * BLOCK], f32))

        def bank(name):
            return ctx.enter_context(nc.psum_tensor(name, [P, BLOCK], f32))

        def sem(name):
            return ctx.enter_context(nc.semaphore(name))

        raw = sb("raw", [P, RAW_SLOTS, TILES * BLOCK])
        mat_hi = sb("mat_hi", [P, SPLIT_SLOTS, GRANULE], f32r)
        mat_lo = sb("mat_lo", [P, SPLIT_SLOTS, GRANULE], f32r)
        u_hi = [sb(f"u_hi{k}", [P, NODES], f32r) for k in range(2)]
        u_lo = [sb(f"u_lo{k}", [P, NODES], f32r) for k in range(2)]
        partial = sb("partial", [P, HALF * BLOCK])
        x_res = sb("x_res", [P, NODES])
        row_sums = sb("row_sums", [P, NODES])
        u_own = row_sums
        col_sums = sb("col_sums", [P, NODE_TILES, BLOCKS])
        out_t = sb("out_t", [P, BLOCK])
        pre_t = sb("pre_t", [P, BLOCK])
        act_t = sb("act_t", [P, BLOCK])
        sum_n = sb("sum_n", [P, BLOCK])
        conv_n = sb("conv_n", [P, BLOCK])
        x_bias = sb("x_bias", [P, BLOCK])
        normed_n = sb("normed_n", [P, BLOCK])
        normed_t = sb("normed_t", [P, BLOCK])
        stats = sb("stats", [P, TILES, 6])
        moments = sb("moments", [P, TILES, 2])
        wait_carrier = sb("wait_carrier", [P, 1])
        var_eps = sb("var_eps", [P, TILES])
        root = sb("root", [P, TILES])
        inv_root = sb("inv_root", [P, TILES])
        newton = sb("newton", [P, TILES])
        better_root = sb("better_root", [P, TILES])
        rstd = sb("rstd", [P, TILES])
        scale_out = sb("scale_out", [P, TILES])
        scale_in = sb("scale_in", [P, TILES])
        degree = sb("degree", [P, NODE_TILES])
        is_zero = sb("is_zero", [P, NODE_TILES])
        degree_safe = sb("degree_safe", [P, NODE_TILES])
        not_zero = sb("not_zero", [P, NODE_TILES])
        degree_root = sb("degree_root", [P, NODE_TILES])
        degree_inv = sb("degree_inv", [P, NODE_TILES])
        degree_work = sb("degree_work", [P, NODE_TILES])
        degree_better = sb("degree_better", [P, NODE_TILES])
        root_or_zero = sb("root_or_zero", [P, NODE_TILES])
        conv1_scale = sb("conv1_scale", [P, NODE_TILES])
        conv2_scale = sb("conv2_scale", [P, NODE_TILES])
        col_sum = sb("col_sum", [P, NODE_TILES])
        col_zero = sb("col_zero", [P, NODE_TILES])
        col_safe = sb("col_safe", [P, NODE_TILES])
        col_inv = sb("col_inv", [P, NODE_TILES])
        col_not = sb("col_not", [P, NODE_TILES])
        hyper_scale = sb("hyper_scale", [P, NODE_TILES])
        w = sb("w", [P, 8, FEATURES])
        b_mlp = sb("b_mlp", [P, 6])
        b_conv = sb("b_conv", [P, TILES + 1, FEATURES])
        ident = sb("ident", [P, P])
        ones = sb("ones", [P, 1])
        pool_scratch = sb("pool_scratch", [P, 1])

        acc = bank_pair("acc")
        part = bank_pair("part")
        dense = [bank("dense0"), bank("dense1")]
        natural = bank("natural")
        projected = bank("projected")

        raw_loaded = [sem(f"raw_loaded{k}") for k in range(RAW_SLOTS)]
        x_loaded = [sem(f"x_loaded{k}") for k in range(BLOCKS)]
        constants_loaded = sem("constants_loaded")
        ones_set = sem("ones_set")
        hi_done = sem("hi_done")
        lo_done = sem("lo_done")
        granule_used = sem("granule_used")
        row_added = sem("row_added")
        evacuated = sem("evacuated")
        part_free = sem("part_free")
        dense_done = [sem(f"dense_done{k}") for k in range(3)]
        pre_ready = [sem(f"pre_ready{k}") for k in range(3)]
        act_ready = [sem(f"act_ready{k}") for k in range(3)]
        natural_done = sem("natural_done")
        u_hi_ready = sem("u_hi_ready")
        u_ready = sem("u_ready")
        scale_out_ready = sem("scale_out_ready")
        scale_in_ready = sem("scale_in_ready")
        u_own_ready = sem("u_own_ready")
        x_bias_ready = sem("x_bias_ready")
        var_ready = sem("var_ready")
        root_ready = sem("root_ready")
        rstd_ready = sem("rstd_ready")
        normed = sem("normed")
        turned_done = sem("turned_done")
        turned_ready = sem("turned_ready")
        project_done = sem("project_done")
        saved = sem("saved")
        vector_step = sem("vector_step")
        degree_step = sem("degree_step")
        x_hi_ready = sem("x_hi_ready")
        x_split = sem("x_split")
        degree_summed = sem("degree_summed")
        degree_safe_ready = sem("degree_safe_ready")
        degree_root_ready = sem("degree_root_ready")
        degrees_ready = sem("degrees_ready")
        out_stored = sem("out_stored")

        def cols(block):
            return ds(block * BLOCK, BLOCK)

        def tile(t):
            return slice(t * P, (t + 1) * P)

        def bank_of(pair, n):
            return pair[:, ds((n & 1) * BLOCK, BLOCK)]

        def part_turn(turn):
            return before(turn.group, lambda g: 1 if g.shared else 0) + turn.i

        def partial_cols(turn):
            low = HALF if max(turn.group.first_out, turn.group.first_out + turn.group.step) >= HALF else 0
            return cols(turn.out - low)

        def is_counted(turn, k):
            return k < turn.granules and k // GRANULES_PER_BLOCK in turn.group.counted

        CONSTANTS = 16 * (3 + TILES + 1)

        block = ctx.enter_context(nc.Block())

        @block.sync
        def _(sp):
            def load_x(c):
                sp.dma_start(x_res[:, c * BLOCK:(c + 1) * BLOCK],
                             stream[c // TILES, :, (c % TILES) * BLOCK:(c % TILES + 1) * BLOCK])\
                  .then_inc(x_loaded[c], 16)

            def turn_loads(turn):
                first = ADJ if turn.group.sweep == len(KINDS) - 1 else ADJ_T
                for place, jb in enumerate(blocks_of(turn.group)):
                    if turn.fresh and turn.group.sweep == 0 and place <= RAW_SLOTS:
                        for c in range(place, place + 1 if place < RAW_SLOTS else BLOCKS):
                            load_x(c)
                    number = turn.block0 + place
                    slot = place % RAW_SLOTS
                    if not (isinstance(number, int) and number < RAW_SLOTS):
                        sp.wait_ge(lo_done, GRANULES_PER_BLOCK * (number - RAW_SLOTS + 1))
                    sp.dma_start(raw[:, slot, :],
                                 stream[ds(turn.out * BLOCKS + (first + jb), 1), :, :].rearrange("o p n -> (o p) n"))\
                      .then_inc(raw_loaded[slot], 16)

            run_turns(sp, turn_loads)

        @block.gpsimd
        def _(pool):
            nc.gpsimd.memset(ones[:], 1.0).then_inc(ones_set, 1)
            pool.wait_ge(ones_set, 1)
            nc.gpsimd.memset(row_sums[:], 0.0).then_inc(row_added, 1)
            nc.gpsimd.memset(normed_n[:, 0:1], 0.0).then_inc(saved, 1)
            for sweep in range(KINDS.index(MLP_LAST), len(KINDS)):
                group = GROUPS[2 * sweep]
                with pool.Fori(0, BLOCKS) as i:
                    tail = BLOCKS * sweep - FIRST_NORMED + i
                    out_block = group.first_out + group.step * i
                    if KINDS[sweep] == CONV_1:
                        pool.wait_ge(normed, tail)
                        pool.wait_ge(saved, tail + 1)
                        nc.gpsimd.tensor_tensor(x_bias[:], x_res[:, cols(out_block)],
                                                b_conv[:, 0:TILES, :].rearrange("p t f -> p (t f)"),
                                                ALU.add).then_inc(x_bias_ready, 1)
                    pool.wait_ge(normed, tail + 1)
                    if KINDS[sweep] == CONV_1:
                        nc.gpsimd.tensor_tensor(pool_scratch[:], ones[:], ones[:], ALU.add)
                    if KINDS[sweep] != HYPER:
                        nc.gpsimd.tensor_copy(x_res[:, cols(out_block)], normed_n[:]).then_inc(saved, 1)
                    else:
                        pool.dma_start(out[ds(out_block, 1), :, :].rearrange("o p n -> (o p) n"),
                                       normed_n[:]).then_inc(out_stored, 16)
                        pool.wait_ge(out_stored, 16 * (i + 1))
                        nc.gpsimd.tensor_tensor(pool_scratch[:], ones[:], ones[:], ALU.add).then_inc(saved, 1)
            pool.wait_ge(out_stored, 16 * BLOCKS)

        @block.scalar
        def _(act):
            def granule(turn, k):
                number = turn.granule0 + k
                block_place = k // GRANULES_PER_BLOCK
                slot = block_place % RAW_SLOTS
                if k % GRANULES_PER_BLOCK == 0:
                    act.wait_ge(raw_loaded[slot], 16 * (turn_block_round(turn) + block_place // RAW_SLOTS + 1))
                if not (isinstance(number, int) and number < SPLIT_SLOTS):
                    act.wait_ge(granule_used, number - SPLIT_SLOTS + 1)
                start = (k % GRANULES_PER_BLOCK) * GRANULE
                if not is_counted(turn, k):
                    nc.scalar.activation(mat_hi[:, k % SPLIT_SLOTS, :], raw[:, slot, start:start + GRANULE],
                                         ACT.Copy).then_inc(hi_done, 1)
                    return
                for t in range(GRANULE_TILES):
                    jt = blocks_of(turn.group)[block_place] * TILES + (k % GRANULES_PER_BLOCK) * GRANULE_TILES + t
                    done = nc.scalar.activation(
                        mat_hi[:, k % SPLIT_SLOTS, t * BLOCK:(t + 1) * BLOCK],
                        raw[:, slot, start + t * BLOCK:start + (t + 1) * BLOCK], ACT.Copy,
                        accum_out=col_sums[:, jt, ds(turn.out, 1)])
                done.then_inc(hi_done, 1)

            def turn_block_round(turn):
                g = turn.group
                return before(g, lambda q: len(blocks_of(q))) // RAW_SLOTS + turn.i * (len(blocks_of(g)) // RAW_SLOTS)

            def tail_step(tail, step):
                e, kind = tail.n, tail.kind
                norm_tail = e - FIRST_NORMED
                if step in ("leaky1", "leaky2", "leaky3"):
                    k = int(step[-1]) - 1
                    bias = (tail.sweep % 2) * 3 + k
                    act.wait_ge(dense_done[k], e + 1)
                    nc.scalar.activation(pre_t[:], dense[k % 2][:], ACT.Identity,
                                         bias=b_mlp[:, bias:bias + 1]).then_inc(pre_ready[k], 1)
                elif step == "scale_out":
                    act.wait_ge(normed, norm_tail)
                    table = {CONV_1: conv1_scale, CONV_2: conv2_scale, HYPER: hyper_scale}[kind]
                    nc.scalar.activation(scale_out[:], table[:, ds(tail.out * TILES, TILES)],
                                         ACT.Copy).then_inc(scale_out_ready, 1)
                elif step == "scale_in":
                    if kind == MLP_LAST:
                        act.wait_ge(degrees_ready, 1)
                    table = {MLP_LAST: conv1_scale, CONV_1: conv2_scale}[kind]
                    if norm_tail_is_first(norm_tail):
                        made = nc.scalar.activation(scale_in[:], table[:, ds(tail.out * TILES, TILES)], ACT.Copy)
                    else:
                        act.wait_ge(u_own_ready, norm_tail)
                        made = nc.scalar.activation(scale_in[:], table[:, ds(tail.out * TILES, TILES)], ACT.Copy)
                    made.then_inc(scale_in_ready, 1)
                elif step == "root":
                    act.wait_ge(var_ready, norm_tail + 1)
                    nc.scalar.activation(root[:], var_eps[:], ACT.Sqrt).then_inc(root_ready, 1)
                elif step == "turned":
                    act.wait_ge(turned_done, norm_tail + 1)
                    nc.scalar.activation(normed_t[:], dense[1][:], ACT.Copy).then_inc(turned_ready, 1)
                elif step == "operand":
                    target = u_hi[(tail.sweep + 1) % 2]
                    if kind == MLP_U:
                        act.wait_ge(natural_done, e + 1)
                        source = natural[:]
                    elif kind == CONV_2:
                        act.wait_ge(normed, norm_tail + 1)
                        source = normed_n[:]
                    else:
                        act.wait_ge(project_done, norm_tail + 1)
                        act.wait_ge(scale_in_ready, norm_tail + 1)
                        for c in range(TILES):
                            done = nc.scalar.activation(
                                u_own[:, ds(tail.out * BLOCK + c * P, P)], projected[:, tile(c)],
                                ACT.Copy, scale=scale_in[:, c:c + 1])
                        done.then_inc(u_own_ready, 1)
                        act.wait_ge(u_own_ready, norm_tail + 1)
                        source = u_own[:, cols(tail.out)]
                    nc.scalar.activation(target[:, cols(tail.out)], source, ACT.Copy).then_inc(u_hi_ready, 1)

            def norm_tail_is_first(norm_tail):
                return isinstance(norm_tail, int) and norm_tail == 0

            def load_constants():
                act.dma_start(b_mlp[:], mlp_biases).then_inc(constants_loaded, 16)
                act.dma_start(w[:], weights).then_inc(constants_loaded, 16)
                act.dma_start(ident[:], identity).then_inc(constants_loaded, 16)
                for k in range(TILES + 1):
                    act.dma_start(b_conv[:, k, :], conv_biases[k // TILES, :].partition_broadcast(P))\
                       .then_inc(constants_loaded, 16)

            def split_turn(turn):
                order = ("scale_out", "scale_in", "leaky1", "leaky2", "leaky3", "root", "turned", "operand")
                for k in range(LEAD, turn.granules + LEAD + 1):
                    for tail, step in steps_at(turn, split_places, order, k):
                        tail_step(tail, step)
                    if k < turn.granules + (0 if turn.last else LEAD):
                        granule(turn, k)
                if not turn.group.adds_partial:
                    act.wait_ge(granule_used, turn.granule0 + turn.granules)
                    nc.scalar.activation(out_t[:], bank_of(acc, turn.n), ACT.Copy).then_inc(evacuated, 1)
                if isinstance(turn.n, int) and turn.n == 0:
                    act.wait_ge(constants_loaded, CONSTANTS)
                if turn.group.shared:
                    act.wait_ge(granule_used, turn.granule0 + turn.granules)
                    nc.scalar.activation(partial[:, partial_cols(turn)], bank_of(part, turn.n),
                                         ACT.Copy).then_inc(part_free, 1)
                if isinstance(turn.n, int) and turn.n == DEGREE_TURN:
                    act.wait_ge(degree_safe_ready, 1)
                    nc.scalar.activation(degree_root[:], degree_safe[:], ACT.Sqrt).then_inc(degree_root_ready, 1)

            first = turn_of(GROUPS[0], 0)

            def split_x(c):
                act.wait_ge(x_loaded[c], 16)
                done = nc.scalar.activation(u_hi[0][:, c * BLOCK:(c + 1) * BLOCK],
                                            x_res[:, c * BLOCK:(c + 1) * BLOCK], ACT.Copy)
                done.then_inc(x_hi_ready, 1)

            split_x(0)
            for k in range(LEAD):
                granule(first, k)
                split_x(k + 1)
            for c in range(LEAD + 1, BLOCKS):
                split_x(c)
            load_constants()
            nc.scalar.activation(root[:], x_res[:, 0:TILES], ACT.Copy).then_inc(part_free, 2)
            run_turns(act, split_turn)
            finale, = turn_of(GROUPS[-1], HALF).tails
            for step in ("scale_out", "root"):
                tail_step(finale, step)

        @block.vector
        def _(dve):
            def granule(turn, k):
                number = turn.granule0 + k
                slot = (k // GRANULES_PER_BLOCK) % RAW_SLOTS
                start = (k % GRANULES_PER_BLOCK) * GRANULE
                dve.wait_ge(hi_done, number + 1)
                if is_counted(turn, k):
                    g = turn.group
                    adds_before = (before(g, lambda q: len(q.counted) * TILES)
                                   + turn.i * len(g.counted) * TILES
                                   + sorted(g.counted).index(k // GRANULES_PER_BLOCK) * TILES
                                   + (k % GRANULES_PER_BLOCK) * GRANULE_TILES)
                    for t in range(GRANULE_TILES):
                        dve.wait_ge(row_added, adds_before + t + 1)
                        nc.vector.tensor_tensor(row_sums[:, cols(turn.out)], row_sums[:, cols(turn.out)],
                                                raw[:, slot, start + t * BLOCK:start + (t + 1) * BLOCK],
                                                ALU.add).then_inc(row_added, 1)
                nc.vector.tensor_tensor(mat_lo[:, k % SPLIT_SLOTS, :], raw[:, slot, start:start + GRANULE],
                                        mat_hi[:, k % SPLIT_SLOTS, :].bitcast(f32),
                                        ALU.subtract).then_inc(lo_done, 1)

            def tail_step(tail, step, count):
                e, kind, where = tail.n, tail.kind, tail.out
                norm_tail = e - FIRST_NORMED
                there = (tail.sweep + 1) % 2

                def signalled(instruction):
                    count[0] += 1
                    instruction.then_inc(vector_step, 1)

                def wait_own():
                    dve.wait_ge(vector_step, vector_steps_before(tail) + count[0])

                if step in ("leaky1", "leaky2", "leaky3"):
                    k = int(step[-1]) - 1
                    dve.wait_ge(pre_ready[k], e + 1)
                    nc.vector.scalar_tensor_tensor(act_t[:], pre_t[:], LEAK, pre_t[:], ALU.mult,
                                                   ALU.max).then_inc(act_ready[k], 1)
                elif step == "moments":
                    dve.wait_ge(natural_done, e + 1)
                    x_here = x_res[:, cols(where)]
                    if kind != MLP_LAST:
                        dve.wait_ge(saved, norm_tail + 1)
                    if kind == MLP_LAST:
                        signalled(nc.vector.tensor_tensor(sum_n[:], natural[:], x_here, ALU.add))
                    elif kind in (CONV_1, CONV_2):
                        signalled(nc.vector.tensor_tensor(conv_n[:], natural[:], u_own[:, cols(where)], ALU.add))
                        wait_own()
                        dve.wait_ge(scale_out_ready, e - FIRST_SCALED + 1)
                        if kind == CONV_1:
                            dve.wait_ge(x_bias_ready, e - FIRST_SCALED + 1)
                        for c in range(TILES):
                            signalled(nc.vector.scalar_tensor_tensor(
                                sum_n[:, tile(c)], conv_n[:, tile(c)], scale_out[:, c:c + 1],
                                x_bias[:, tile(c)] if kind == CONV_1 else b_conv[:, TILES, :],
                                ALU.mult, ALU.add))
                        if kind == CONV_2:
                            wait_own()
                            signalled(nc.vector.scalar_tensor_tensor(sum_n[:], sum_n[:], 0.0, x_here,
                                                                     ALU.max, ALU.add))
                    else:
                        dve.wait_ge(scale_out_ready, e - FIRST_SCALED + 1)
                        for c in range(TILES):
                            signalled(nc.vector.scalar_tensor_tensor(
                                sum_n[:, tile(c)], natural[:, tile(c)], scale_out[:, c:c + 1],
                                x_res[:, ds(where * BLOCK + c * P, P)], ALU.mult, ALU.add))
                    wait_own()
                    for c in range(TILES):
                        signalled(nc.vector.bn_stats(stats[:, c, :], sum_n[:, tile(c)]))
                    wait_own()
                    nc.vector.memset(wait_carrier[:], 0.0)
                    for c in range(TILES):
                        signalled(nc.vector.bn_aggr(moments[:, c, :], stats[:, c, :]))
                    wait_own()
                    nc.vector.tensor_scalar(var_eps[:], moments[:, :, 1], LN_EPS, None,
                                            ALU.add).then_inc(var_ready, 1)
                elif step == "norm":
                    dve.wait_ge(root_ready, norm_tail + 1)
                    signalled(nc.vector.reciprocal(inv_root[:], root[:]))
                    wait_own()
                    signalled(nc.vector.scalar_tensor_tensor(newton[:], var_eps[:], 0.5, inv_root[:],
                                                             ALU.mult, ALU.mult))
                    wait_own()
                    signalled(nc.vector.scalar_tensor_tensor(better_root[:], root[:], 0.5, newton[:],
                                                             ALU.mult, ALU.add))
                    wait_own()
                    dve.wait_ge(saved, norm_tail + 1)
                    turned = KINDS.index(CONV_2) * BLOCKS - FIRST_NORMED
                    if kind in LONG_TAILS and not (isinstance(norm_tail, int) and norm_tail == 0):
                        dve.wait_ge(turned_done, norm_tail)
                    elif kind not in LONG_TAILS:
                        dve.wait_ge(turned_done, turned)
                    rstd_made = nc.vector.reciprocal(rstd[:], better_root[:])
                    rstd_made.then_inc(rstd_ready, 1)
                    dve.wait_ge(rstd_ready, norm_tail + 1)
                    for c in range(TILES):
                        done = nc.vector.tensor_scalar(normed_n[:, tile(c)], sum_n[:, tile(c)],
                                                       moments[:, c, 0:1], rstd[:, c:c + 1],
                                                       ALU.subtract, ALU.mult)
                    done.then_inc(normed, 1)
                    assert count[0] == VECTOR_STEPS[kind], (kind, count[0])
                elif step == "operand":
                    dve.wait_ge(u_hi_ready, e + 1)
                    high, low = u_hi[there], u_lo[there]
                    source = {MLP_U: natural[:], CONV_2: normed_n[:]}.get(kind, u_own[:, cols(where)])
                    nc.vector.tensor_tensor(low[:, cols(where)], source, high[:, cols(where)].bitcast(f32),
                                            ALU.subtract).then_inc(u_ready, 1)

            def degrees():
                steps = [0]

                def chained(instruction):
                    steps[0] += 1
                    instruction.then_inc(degree_step, 1)
                    dve.wait_ge(degree_step, steps[0])

                dve.wait_ge(degree_summed, 1)
                chained(nc.vector.tensor_scalar(degree[:], projected[:, 0:NODE_TILES], 1.0, None, ALU.add))
                chained(nc.vector.tensor_scalar(is_zero[:], degree[:], 0.0, None, ALU.is_equal))
                nc.vector.tensor_tensor(degree_safe[:], degree[:], is_zero[:], ALU.add)\
                  .then_inc(degree_safe_ready, 1)
                chained(nc.vector.tensor_scalar(not_zero[:], is_zero[:], -1.0, 1.0, ALU.mult, ALU.add))
                chained(nc.vector.tensor_reduce(col_sum[:], col_sums[:], AX.X, ALU.add))
                chained(nc.vector.tensor_scalar(col_zero[:], col_sum[:], 0.0, None, ALU.is_equal))
                chained(nc.vector.tensor_tensor(col_safe[:], col_sum[:], col_zero[:], ALU.add))
                chained(nc.vector.tensor_scalar(col_not[:], col_zero[:], -1.0, 1.0, ALU.mult, ALU.add))
                chained(nc.vector.reciprocal(col_inv[:], col_safe[:]))
                chained(nc.vector.tensor_tensor(hyper_scale[:], col_inv[:], col_not[:], ALU.mult))
                dve.wait_ge(degree_root_ready, 1)
                chained(nc.vector.reciprocal(degree_inv[:], degree_root[:]))
                chained(nc.vector.scalar_tensor_tensor(degree_work[:], degree_safe[:], 0.5, degree_inv[:],
                                                       ALU.mult, ALU.mult))
                chained(nc.vector.scalar_tensor_tensor(degree_better[:], degree_root[:], 0.5, degree_work[:],
                                                       ALU.mult, ALU.add))
                chained(nc.vector.tensor_tensor(root_or_zero[:], degree_better[:], not_zero[:], ALU.mult))
                chained(nc.vector.reciprocal(conv2_scale[:], root_or_zero[:]))
                chained(nc.vector.reciprocal(degree_inv[:], degree_better[:]))
                nc.vector.tensor_tensor(conv1_scale[:], degree_inv[:], not_zero[:], ALU.mult)\
                  .then_inc(degrees_ready, 1)

            def split_turn(turn):
                order = ("leaky1", "leaky2", "leaky3", "moments", "norm", "operand")
                counts = {tail.stage: [0] for tail in turn.tails}
                for k in range(LEAD, turn.granules + LEAD + 1):
                    for tail, step in steps_at(turn, split_places, order, k):
                        tail_step(tail, step, counts[tail.stage])
                    if k < turn.granules + (0 if turn.last else LEAD):
                        granule(turn, k)
                if turn.group.adds_partial:
                    dve.wait_ge(granule_used, turn.granule0 + turn.granules)
                    nc.vector.tensor_tensor(out_t[:], bank_of(acc, turn.n), partial[:, partial_cols(turn)],
                                            ALU.add).then_inc(evacuated, 1)
                if isinstance(turn.n, int) and turn.n == DEGREE_TURN:
                    degrees()

            first = turn_of(GROUPS[0], 0)

            def split_x(c):
                dve.wait_ge(x_hi_ready, c + 1)
                here = slice(c * BLOCK, (c + 1) * BLOCK)
                nc.vector.tensor_tensor(u_lo[0][:, here], x_res[:, here], u_hi[0][:, here].bitcast(f32),
                                        ALU.subtract).then_inc(x_split, 1)
                if c == BLOCKS - 1:
                    dve.wait_ge(x_split, BLOCKS)
                    nc.vector.memset(inv_root[:], 0.0).then_inc(u_ready, 1)

            split_x(0)
            for k in range(LEAD):
                granule(first, k)
                split_x(k + 1)
            for c in range(LEAD + 1, BLOCKS):
                split_x(c)
            nc.vector.memset(newton[:], 0.0).then_inc(evacuated, 1)
            run_turns(dve, split_turn)
            finale, = turn_of(GROUPS[-1], HALF).tails
            count = [0]
            for step in ("moments", "norm"):
                tail_step(finale, step, count)

        @block.tensor
        def _(pe):
            def tail_step(tail, step):
                e, kind = tail.n, tail.kind
                norm_tail = e - FIRST_NORMED
                if step in ("dense1", "dense2", "dense3"):
                    k = int(step[-1]) - 1
                    if k == 0:
                        pe.wait_ge(evacuated, e + 2)
                    else:
                        pe.wait_ge(act_ready[k - 1], e + 1)
                    nc.tensor.matmul(dense[k % 2][:], w[:, (tail.sweep % 2) * 3 + k, :], (act_t if k else out_t)[:],
                                     start=True, stop=True).then_inc(dense_done[k], 1)
                elif step == "natural":
                    if kind in (MLP_U, MLP_LAST):
                        pe.wait_ge(act_ready[2], e + 1)
                    else:
                        pe.wait_ge(evacuated, e + 2)
                    if kind == MLP_U or isinstance(norm_tail, int) and norm_tail == 0:
                        pe.wait_ge(u_ready, e + 1)
                    else:
                        pe.wait_ge(normed, norm_tail)
                    source = act_t if kind in (MLP_U, MLP_LAST) else out_t
                    for c in range(TILES):
                        done = nc.tensor.transpose(natural[:, tile(c)], source[:, tile(c)], ident[:])
                    done.then_inc(natural_done, 1)
                elif step == "turn_x":
                    pe.wait_ge(normed, norm_tail + 1)
                    for c in range(TILES):
                        done = nc.tensor.transpose(dense[1][:, tile(c)], normed_n[:, tile(c)], ident[:])
                    done.then_inc(turned_done, 1)
                elif step == "project":
                    pe.wait_ge(turned_ready, norm_tail + 1)
                    if kind == MLP_LAST:
                        pe.wait_ge(degrees_ready, 1)
                    if not (isinstance(norm_tail, int) and norm_tail == 0):
                        pe.wait_ge(u_own_ready, norm_tail)
                    for c in range(TILES):
                        done = nc.tensor.matmul(projected[:, tile(c)], normed_t[:, tile(c)],
                                                w[:, 6 if kind == MLP_LAST else 7, :], start=True, stop=True)
                    done.then_inc(project_done, 1)

            def sum_degrees():
                counted = sum(HALF * TILES * len(g.counted) for g in GROUPS)
                assert counted == BLOCKS * NODE_TILES
                pe.wait_ge(row_added, counted + 1)
                pe.wait_ge(ones_set, 1)
                for t in range(NODE_TILES):
                    done = nc.tensor.matmul(projected[:, t:t + 1], row_sums[:, tile(t)], ones[:],
                                            start=True, stop=True)
                done.then_inc(degree_summed, 1)

            def products(turn):
                group, n = turn.group, turn.n
                here, there = group.sweep % 2, (group.sweep + 1) % 2
                if not (isinstance(n, int) and n == 0):
                    pe.wait_ge(evacuated, n)
                    if turn.fresh:
                        pe.wait_ge(u_ready, n)
                if group.shared:
                    pe.wait_ge(part_free, part_turn(turn) + 1)
                acc_out, part_out = bank_of(acc, n), bank_of(part, n)
                last_place = len(blocks_of(group)) - 1
                for k in range(turn.granules):
                    place = k // GRANULES_PER_BLOCK
                    jb, shared = blocks_of(group)[place], bool(group.shared) and place % 2 == 1
                    if k % GRANULES_PER_BLOCK == 0:
                        if isinstance(n, int) and n == 0:
                            pe.wait_ge(x_split, place + 1)
                        elif place == last_place and (turn.fresh or group.shared):
                            pe.wait_ge(u_ready, n + 1)
                    pe.wait_ge(lo_done, turn.granule0 + k + 1)
                    for target, parity in ((acc_out, here), (part_out, there))[:1 + shared]:
                        first_place = 1 if target is part_out else 0
                        for t in range(GRANULE_TILES):
                            jt = jb * TILES + (k % GRANULES_PER_BLOCK) * GRANULE_TILES + t
                            start = place == first_place and k % GRANULES_PER_BLOCK == 0 and t == 0
                            stop = k == turn.granules - 1 and t == GRANULE_TILES - 1
                            strip = slice(t * BLOCK, (t + 1) * BLOCK)
                            hi, lo = mat_hi[:, k % SPLIT_SLOTS, strip], mat_lo[:, k % SPLIT_SLOTS, strip]
                            nc.tensor.matmul(target, u_hi[parity][:, tile(jt)], hi, start=start, stop=False)
                            nc.tensor.matmul(target, u_hi[parity][:, tile(jt)], lo, start=False, stop=False)
                            done = nc.tensor.matmul(target, u_lo[parity][:, tile(jt)], hi,
                                                    start=False, stop=stop)
                    done.then_inc(granule_used, 1)
                    if isinstance(n, int) and n == 0 and k == turn.granules - 1:
                        pe.wait_ge(constants_loaded, CONSTANTS)
                    order = ("dense1", "dense2", "dense3", "natural", "turn_x", "project")
                    for tail, step in steps_at(turn, tensor_places, order, k):
                        tail_step(tail, step)
                    if k == LEAD and isinstance(n, int) and n == DEGREE_TURN:
                        sum_degrees()

            run_turns(pe, products)
            tail_step(turn_of(GROUPS[-1], HALF).tails[0], "natural")


def kernel(x, adj, L0_gnn_v_node_feats, L0_gnn_uv_W1, L0_gnn_uv_b1, L0_gnn_uv_W2, L0_gnn_uv_b2,
           L0_gnn_uv_W3, L0_gnn_uv_b3, L0_gnn_vu_W1, L0_gnn_vu_b1, L0_gnn_vu_W2, L0_gnn_vu_b2,
           L0_gnn_vu_W3, L0_gnn_vu_b3, L1_gnn_W, L1_gnn_b, L2_gnn_W, L2_gnn_b):
    import numpy as np
    import concourse.bacc as bacc
    from concourse.bass_utils import run_bass_kernel_spmd

    a, x = np.asarray(adj), np.asarray(x)
    strip = (-1, P, TILES * BLOCK)
    arrays = {
        "stream": np.concatenate([
            x.reshape(ADJ_T, -1, P, FEATURES).transpose(0, 2, 1, 3).reshape(strip),
            a.reshape(BLOCKS, BLOCK, BLOCKS, TILES, P).transpose(0, 2, 4, 3, 1).reshape(strip),
            a.reshape(BLOCKS, TILES, P, BLOCKS, BLOCK).transpose(3, 0, 2, 1, 4).reshape(strip)]),
        "weights": np.stack([np.asarray(m) for m in (
            L0_gnn_uv_W1, L0_gnn_uv_W2, L0_gnn_uv_W3, L0_gnn_vu_W1, L0_gnn_vu_W2, L0_gnn_vu_W3,
            np.asarray(L1_gnn_W).T, L2_gnn_W)], axis=1),
        "mlp_biases": np.stack([np.asarray(b) for b in (
            L0_gnn_uv_b1, L0_gnn_uv_b2, L0_gnn_uv_b3, L0_gnn_vu_b1, L0_gnn_vu_b2, L0_gnn_vu_b3)], axis=1),
        "conv_biases": np.stack([np.asarray(L1_gnn_b), np.asarray(L2_gnn_b)]),
        "identity": np.eye(P, dtype=np.float32),
    }
    arrays = {name: np.ascontiguousarray(value) for name, value in arrays.items()}
    nc = bacc.Bacc("TRN2", target_bir_lowering=False, num_devices=1)
    args = [nc.dram_tensor(name, v.shape, mybir.dt.from_np(v.dtype), kind="ExternalInput").ap()
            for name, v in arrays.items()]
    out = nc.dram_tensor("out_blocks", (BLOCKS, P, BLOCK), mybir.dt.float32, kind="ExternalOutput").ap()
    gnn_stack(nc, *args, out)
    got = run_bass_kernel_spmd(nc, [arrays], core_ids=[0]).results[0]["out_blocks"]
    return got.reshape(BLOCKS, P, TILES, FEATURES).transpose(0, 2, 1, 3).reshape(NODES, FEATURES)
```

```python
from contextlib import ExitStack
from collections import namedtuple

import concourse.bass as bass
from concourse import mybir

NODES, FEATURES = 4096, 128
P = 128
BLOCK = 512
BLOCKS = NODES // BLOCK
HALF = BLOCKS // 2
TILES = BLOCK // P
NODE_TILES = NODES // P
GRANULE_TILES = 2
GRANULE = GRANULE_TILES * BLOCK
GRANULES_PER_BLOCK = TILES // GRANULE_TILES
RAW_SLOTS = 4
SPLIT_SLOTS = 4
LEAD = 3
ADJ_T = NODES // (TILES * BLOCK)
ADJ = ADJ_T + BLOCKS * BLOCKS
ROWS, LO_ROW = 64, 32
LN_EPS = 1e-5
LEAK = 0.01

MLP_U, MLP_LAST, CONV_1, CONV_2, HYPER = range(5)
KINDS = [MLP_U, MLP_U, MLP_U, MLP_U, MLP_LAST, CONV_1, CONV_2, HYPER]
FIRST_NORMED = BLOCKS * KINDS.index(MLP_LAST)
FIRST_SCALED = BLOCKS * KINDS.index(CONV_1)
DEGREE_TURN = FIRST_NORMED
DEGREE_PLACE = 5

Group = namedtuple("Group", "sweep second first_out step own shared counted adds_partial")
GROUPS = [
    Group(0, 0, 0, +1, (0, 1, 2, 3, 4, 5, 6, 7), (), (), False),
    Group(0, 1, 4, +1, (4, 5, 6, 7), (0, 1, 2, 3), (2, 4, 5, 7), False),
    Group(1, 0, 7, -1, (4, 5, 6, 7), (), (), True),
    Group(1, 1, 3, -1, (0, 1, 2, 3), (7, 6, 5, 4), (2, 4, 5, 7), False),
    Group(2, 0, 0, +1, (3, 2, 1, 0), (), (), True),
    Group(2, 1, 4, +1, (5, 4, 6, 7), (2, 0, 1, 3), (2, 3, 5, 6), False),
    Group(3, 0, 7, -1, (4, 5, 6, 7), (), (), True),
    Group(3, 1, 3, -1, (1, 0, 2, 3), (5, 6, 7, 4), (2, 3, 5, 6), False),
    Group(4, 0, 0, +1, (3, 2, 1, 0), (), (), True),
    Group(4, 1, 4, +1, (4, 5, 6, 7), (0, 1, 2, 3), (), False),
    Group(5, 0, 7, -1, (4, 5, 6, 7), (), (), True),
    Group(5, 1, 3, -1, (0, 1, 2, 3), (7, 6, 5, 4), (), False),
    Group(6, 0, 0, +1, (3, 2, 1, 0), (), (), True),
    Group(6, 1, 4, +1, (0, 1, 2, 3, 4, 5, 6, 7), (), (), False),
    Group(7, 0, 7, -1, (0, 1, 2, 3, 4, 5, 6, 7), (), (), False),
    Group(7, 1, 3, -1, (0, 1, 2, 3, 4, 5, 6, 7), (), (), False),
]


def blocks_of(group):
    if not group.shared:
        return group.own
    return tuple(b for pair in zip(group.own, group.shared) for b in pair)


def granules_of(group):
    return GRANULES_PER_BLOCK * len(blocks_of(group))


def before(group, count):
    return sum(HALF * count(g) for g in GROUPS[:GROUPS.index(group)])


Turn = namedtuple("Turn", "group i n out tails fresh last granules granule0 block0")
Tail = namedtuple("Tail", "kind n out sweep stage")
ALL, FIRST, SECOND = range(3)
LONG_TAILS = (MLP_LAST,)


def turn_of(group, i, last=False):
    sweep, per_turn = group.sweep, granules_of(group)
    fresh = isinstance(i, int) and i == 0 and not group.second
    first_of_group = isinstance(i, int) and i == 0
    n = BLOCKS * sweep + HALF * group.second + i
    out = group.first_out + group.step * i
    tails = []
    if fresh:
        if sweep:
            tails.append(Tail(KINDS[sweep - 1], n - 1, out, sweep - 1, ALL))
    else:
        kind = KINDS[sweep]
        split = kind in LONG_TAILS
        second_turn = isinstance(i, int) and i == 1 and not group.second
        if split and not second_turn and (not group.second or first_of_group):
            tails.append(Tail(kind, n - 2, out - 2 * group.step, sweep, SECOND))
        tails.append(Tail(kind, n - 1, out - group.step, sweep, FIRST if split and not group.second else ALL))
    return Turn(group, i, n, out, tails, fresh, last, per_turn,
                before(group, granules_of) + i * per_turn,
                before(group, lambda g: len(blocks_of(g))) + i * len(blocks_of(group)))


def run_turns(eng, body):
    for group in GROUPS:
        split = KINDS[group.sweep] in LONG_TAILS
        at_end = group is GROUPS[-1]
        start = (int(split) if group.second else 1 + split)
        for i in range(start):
            body(turn_of(group, i))
        with eng.Fori(start, HALF - 1 if at_end else HALF) as i:
            body(turn_of(group, i))
        if at_end:
            body(turn_of(group, HALF - 1, last=True))


def tensor_places(turn, tail):
    if tail.kind in (MLP_U, MLP_LAST):
        if tail.stage == SECOND:
            return {}
        if turn.fresh:
            return {"dense1": -1, "dense2": 1, "natural": 3}
        if turn.group.second and tail.kind == MLP_U:
            return {"dense1": 1, "dense2": 5, "natural": 8}
        return {"dense1": 1, "dense2": 3, "natural": 5}
    return {"natural": -1 if turn.fresh else 1}


def split_places(turn, tail):
    if tail.kind == MLP_U and turn.fresh:
        return {"leaky1": 4, "leaky2": 6, "leaky3": 8, "operand": 8}
    if tail.kind == MLP_U:
        if turn.group.second:
            return {"leaky1": 5, "leaky2": 10, "leaky3": 13, "operand": 15}
        return {"leaky1": 5, "leaky2": 7, "leaky3": 9, "operand": 10}
    if tail.kind == MLP_LAST:
        start = {"leaky1": 4, "leaky2": 7, "leaky3": 9}
        if tail.stage == SECOND:
            return {"scale_in": 4, "sum": 4, "moments": 4, "root": 6, "norm": 6, "normalise": 6, "operand": 8}
        if tail.stage == FIRST:
            return start
        if turn.fresh:
            return {"leaky1": 4, "leaky2": 6, "leaky3": 7, "scale_in": 4, "sum": 7, "moments": 7, "root": 7,
                    "norm": 7, "normalise": 7, "operand": 7}
        return start | {"scale_in": 11, "sum": 10, "moments": 10, "root": 11, "norm": 11, "normalise": 11,
                        "operand": 13}
    if tail.kind in (CONV_1, CONV_2):
        scales = {"scale_out": 3, "scale_in": 3} if tail.kind == CONV_1 else {"scale_out": 3}
        if turn.fresh:
            return scales | {"sum": 3, "moments": 4, "root": 5, "norm": 5, "normalise": 5, "operand": 6}
        if turn.group.second:
            return scales | {"sum": 5, "moments": 7, "root": 9, "norm": 9, "normalise": 11, "operand": 13}
        return scales | {"sum": 5, "moments": 6, "root": 7, "norm": 7, "normalise": 8, "operand": 10}
    return {"scale_out": 3, "sum": 5, "moments": 8, "root": 11, "norm": 11, "normalise": 13}


OWN, FRESH_OWN = 5, 10


def steps_at(turn, places, order, k):
    return [(tail, step) for tail in turn.tails for step in order if places(turn, tail).get(step) == k]


VECTOR_STEPS = {MLP_U: 0, MLP_LAST: 12, CONV_1: 15, CONV_2: 16, HYPER: 15}


def vector_steps_before(tail):
    kinds = KINDS[:tail.sweep]
    return sum(BLOCKS * VECTOR_STEPS[k] for k in kinds) + (tail.n - BLOCKS * tail.sweep) * VECTOR_STEPS[tail.kind]


def gnn_stack(nc, stream, weights, mlp_biases, last_biases, conv_biases, constants, out):
    f32, f32r = mybir.dt.float32, mybir.dt.float32r
    ALU, ACT, AX = mybir.AluOpType, mybir.ActivationFunctionType, mybir.AxisListType
    ds = bass.ds

    ctx = ExitStack()
    with ctx:
        def sb(name, shape, dt=f32):
            return ctx.enter_context(nc.sbuf_tensor(name, shape, dt))

        def bank_pair(name):
            return ctx.enter_context(nc.psum_tensor(name, [P, 2 * BLOCK], f32))

        def bank(name):
            return ctx.enter_context(nc.psum_tensor(name, [P, BLOCK], f32))

        def sem(name):
            return ctx.enter_context(nc.semaphore(name))

        raw = sb("raw", [P, RAW_SLOTS, TILES * BLOCK])
        mat_hi = sb("mat_hi", [P, SPLIT_SLOTS, GRANULE], f32r)
        mat_lo = sb("mat_lo", [P, SPLIT_SLOTS, GRANULE], f32r)
        u_hi = [sb(f"u_hi{k}", [P, NODES], f32r) for k in range(2)]
        u_lo = [sb(f"u_lo{k}", [P, NODES], f32r) for k in range(2)]
        own_hi = sb("own_hi", [P, BLOCK], f32r)
        own_lo = sb("own_lo", [P, BLOCK], f32r)
        partial = sb("partial", [P, HALF * BLOCK])
        x_res = sb("x_res", [P, NODES])
        row_sums = sb("row_sums", [P, NODES])
        col_sums = sb("col_sums", [P, NODE_TILES, BLOCKS])
        out_t = sb("out_t", [P, BLOCK])
        pre_t = sb("pre_t", [P, BLOCK])
        act_t = sb("act_t", [P, BLOCK])
        sum_n = sb("sum_n", [P, BLOCK])
        act_n = sb("act_n", [P, BLOCK])
        x_bias = sb("x_bias", [P, BLOCK])
        normed_n = sb("normed_n", [P, BLOCK])
        stats = sb("stats", [P, TILES, 6])
        moments = sb("moments", [P, TILES, 2])
        wait_carrier = sb("wait_carrier", [P, 1])
        var_eps = sb("var_eps", [P, TILES])
        root = sb("root", [P, TILES])
        inv_root = sb("inv_root", [P, TILES])
        newton = sb("newton", [P, TILES])
        better_root = sb("better_root", [P, TILES])
        rstd = sb("rstd", [P, TILES])
        scale_out = sb("scale_out", [P, TILES])
        scale_in = sb("scale_in", [P, TILES])
        degree = sb("degree", [P, NODE_TILES])
        is_zero = sb("is_zero", [P, NODE_TILES])
        degree_safe = sb("degree_safe", [P, NODE_TILES])
        not_zero = sb("not_zero", [P, NODE_TILES])
        degree_root = sb("degree_root", [P, NODE_TILES])
        degree_inv = sb("degree_inv", [P, NODE_TILES])
        degree_work = sb("degree_work", [P, NODE_TILES])
        degree_better = sb("degree_better", [P, NODE_TILES])
        root_or_zero = sb("root_or_zero", [P, NODE_TILES])
        conv1_scale = sb("conv1_scale", [P, NODE_TILES])
        conv2_scale = sb("conv2_scale", [P, NODE_TILES])
        col_sum = sb("col_sum", [P, NODE_TILES])
        col_zero = sb("col_zero", [P, NODE_TILES])
        col_safe = sb("col_safe", [P, NODE_TILES])
        col_inv = sb("col_inv", [P, NODE_TILES])
        col_not = sb("col_not", [P, NODE_TILES])
        hyper_scale = sb("hyper_scale", [P, NODE_TILES])
        w = sb("w", [P, 8, FEATURES])
        b_mlp = sb("b_mlp", [P, 4])
        b_last = sb("b_last", [ROWS, 2 * BLOCK], f32r)
        b_conv = sb("b_conv", [P, TILES + 1, FEATURES])
        ident = sb("ident", [P, 2 * P])
        ident_r = sb("ident_r", [P, 2 * P], f32r)
        ones = sb("ones", [P, 1])
        pool_scratch = sb("pool_scratch", [P, 1])

        acc = bank_pair("acc")
        part = bank_pair("part")
        dense = [bank("dense0"), bank("dense1")]
        natural = bank("natural")
        degree_sums = bank("degree_sums")

        raw_loaded = [sem(f"raw_loaded{k}") for k in range(RAW_SLOTS)]
        x_loaded = [sem(f"x_loaded{k}") for k in range(BLOCKS)]
        constants_loaded = sem("constants_loaded")
        constants_hi = sem("constants_hi")
        constants_ready = sem("constants_ready")
        ones_set = sem("ones_set")
        hi_done = sem("hi_done")
        lo_done = sem("lo_done")
        granule_used = sem("granule_used")
        row_added = sem("row_added")
        acc_done = sem("acc_done")
        evacuated = sem("evacuated")
        part_free = sem("part_free")
        dense_done = [sem(f"dense_done{k}") for k in range(2)]
        pre_ready = [sem(f"pre_ready{k}") for k in range(3)]
        act_ready = [sem(f"act_ready{k}") for k in range(3)]
        natural_done = sem("natural_done")
        u_hi_ready = sem("u_hi_ready")
        u_ready = sem("u_ready")
        own_ready = sem("own_ready")
        scale_out_ready = sem("scale_out_ready")
        scale_in_ready = sem("scale_in_ready")
        x_bias_ready = sem("x_bias_ready")
        var_ready = sem("var_ready")
        root_ready = sem("root_ready")
        rstd_ready = sem("rstd_ready")
        normed = sem("normed")
        saved = sem("saved")
        vector_step = sem("vector_step")
        degree_step = sem("degree_step")
        x_hi_ready = sem("x_hi_ready")
        x_split = sem("x_split")
        degree_summed = sem("degree_summed")
        degree_safe_ready = sem("degree_safe_ready")
        degree_root_ready = sem("degree_root_ready")
        degrees_ready = sem("degrees_ready")
        out_stored = sem("out_stored")

        def cols(block):
            return ds(block * BLOCK, BLOCK)

        def tile(t):
            return slice(t * P, (t + 1) * P)

        def bank_of(pair, n):
            return pair[:, ds((n & 1) * BLOCK, BLOCK)]

        def part_turn(turn):
            return before(turn.group, lambda g: 1 if g.shared else 0) + turn.i

        def partial_cols(turn):
            low = HALF if max(turn.group.first_out, turn.group.first_out + turn.group.step) >= HALF else 0
            return cols(turn.out - low)

        def has_own(turn):
            return KINDS[turn.group.sweep] in (CONV_1, CONV_2)

        def counting(group):
            counted = [k for k, g in enumerate(GROUPS) if g.counted]
            return int(counted[0] <= GROUPS.index(group) <= counted[-1] + 1)

        def is_counted(turn, k):
            return k < turn.granules and k // GRANULES_PER_BLOCK in turn.group.counted

        CONSTANTS = 16 * (4 + TILES + 1)

        block = ctx.enter_context(nc.Block())

        @block.sync
        def _(sp):
            def load_x(c):
                sp.dma_start(x_res[:, c * BLOCK:(c + 1) * BLOCK],
                             stream[c // TILES, :, (c % TILES) * BLOCK:(c % TILES + 1) * BLOCK])\
                  .then_inc(x_loaded[c], 16)

            def turn_loads(turn):
                first = ADJ if turn.group.sweep == len(KINDS) - 1 else ADJ_T
                for place, jb in enumerate(blocks_of(turn.group)):
                    if isinstance(turn.n, int) and turn.n == 0:
                        load_x(place)
                    number = turn.block0 + place
                    slot = place % RAW_SLOTS
                    if not (isinstance(number, int) and number < RAW_SLOTS):
                        sp.wait_ge(lo_done, GRANULES_PER_BLOCK * (number - RAW_SLOTS + 1) + counting(turn.group))
                    sp.dma_start(raw[:, slot, :],
                                 stream[ds(turn.out * BLOCKS + (first + jb), 1), :, :].rearrange("o p n -> (o p) n"))\
                      .then_inc(raw_loaded[slot], 16)

            run_turns(sp, turn_loads)

        @block.gpsimd
        def _(pool):
            nc.gpsimd.memset(ones[:], 1.0).then_inc(ones_set, 1)
            pool.wait_ge(ones_set, 1)
            nc.gpsimd.memset(row_sums[:], 0.0).then_inc(row_added, 1)
            nc.gpsimd.memset(normed_n[:, 0:1], 0.0).then_inc(saved, 1)
            for sweep in range(KINDS.index(MLP_LAST), len(KINDS)):
                group = GROUPS[2 * sweep]
                with pool.Fori(0, BLOCKS) as i:
                    tail = BLOCKS * sweep - FIRST_NORMED + i
                    out_block = group.first_out + group.step * i
                    if KINDS[sweep] == CONV_1:
                        pool.wait_ge(normed, tail)
                        pool.wait_ge(saved, tail + 1)
                        nc.gpsimd.tensor_tensor(x_bias[:], x_res[:, cols(out_block)],
                                                b_conv[:, 0:TILES, :].rearrange("p t f -> p (t f)"),
                                                ALU.add).then_inc(x_bias_ready, 1)
                    pool.wait_ge(normed, tail + 1)
                    if KINDS[sweep] == CONV_1:
                        nc.gpsimd.tensor_tensor(pool_scratch[:], ones[:], ones[:], ALU.add)
                    if KINDS[sweep] != HYPER:
                        nc.gpsimd.tensor_copy(x_res[:, cols(out_block)], normed_n[:]).then_inc(saved, 1)
                    else:
                        pool.dma_start(out[ds(out_block, 1), :, :].rearrange("o p n -> (o p) n"),
                                       normed_n[:]).then_inc(out_stored, 16)
                        pool.wait_ge(out_stored, 16 * (i + 1))
                        nc.gpsimd.tensor_tensor(pool_scratch[:], ones[:], ones[:], ALU.add).then_inc(saved, 1)
            pool.wait_ge(out_stored, 16 * BLOCKS)

        @block.scalar
        def _(act):
            def granule(turn, k):
                number = turn.granule0 + k
                block_place = k // GRANULES_PER_BLOCK
                slot = block_place % RAW_SLOTS
                if k % GRANULES_PER_BLOCK == 0:
                    act.wait_ge(raw_loaded[slot], 16 * (turn_block_round(turn) + block_place // RAW_SLOTS + 1))
                if not (isinstance(number, int) and number < SPLIT_SLOTS):
                    act.wait_ge(granule_used, number - SPLIT_SLOTS + 1)
                start = (k % GRANULES_PER_BLOCK) * GRANULE
                if not is_counted(turn, k):
                    nc.scalar.activation(mat_hi[:, k % SPLIT_SLOTS, :], raw[:, slot, start:start + GRANULE],
                                         ACT.Copy).then_inc(hi_done, 1)
                    return
                for t in range(GRANULE_TILES):
                    jt = blocks_of(turn.group)[block_place] * TILES + (k % GRANULES_PER_BLOCK) * GRANULE_TILES + t
                    done = nc.scalar.activation(
                        mat_hi[:, k % SPLIT_SLOTS, t * BLOCK:(t + 1) * BLOCK],
                        raw[:, slot, start + t * BLOCK:start + (t + 1) * BLOCK], ACT.Copy,
                        accum_out=col_sums[:, jt, ds(turn.out, 1)])
                done.then_inc(hi_done, 1)

            def turn_block_round(turn):
                g = turn.group
                return before(g, lambda q: len(blocks_of(q))) // RAW_SLOTS + turn.i * (len(blocks_of(g)) // RAW_SLOTS)

            def tail_step(tail, step):
                e, kind = tail.n, tail.kind
                norm_tail = e - FIRST_NORMED
                if step in ("leaky1", "leaky2"):
                    k = int(step[-1]) - 1
                    bias = (tail.sweep % 2) * 2 + k
                    act.wait_ge(dense_done[k], e + 1)
                    nc.scalar.activation(pre_t[:], dense[k % 2][:], ACT.Identity,
                                         bias=b_mlp[:, bias:bias + 1]).then_inc(pre_ready[k], 1)
                elif step == "leaky3":
                    act.wait_ge(natural_done, e + 1)
                    nc.scalar.activation(pre_t[:], natural[:], ACT.Copy).then_inc(pre_ready[2], 1)
                elif step == "scale_out":
                    act.wait_ge(normed, norm_tail)
                    table = {CONV_1: conv1_scale, CONV_2: conv2_scale, HYPER: hyper_scale}[kind]
                    nc.scalar.activation(scale_out[:], table[:, ds(tail.out * TILES, TILES)],
                                         ACT.Copy).then_inc(scale_out_ready, 1)
                elif step == "scale_in":
                    if kind == MLP_LAST:
                        act.wait_ge(degrees_ready, 1)
                    table = {MLP_LAST: conv1_scale, CONV_1: conv2_scale}[kind]
                    act.wait_ge(u_ready, e + 1)
                    nc.scalar.activation(scale_in[:], table[:, ds(tail.out * TILES, TILES)],
                                         ACT.Copy).then_inc(scale_in_ready, 1)
                elif step == "root":
                    act.wait_ge(var_ready, norm_tail + 1)
                    nc.scalar.activation(root[:], var_eps[:], ACT.Sqrt).then_inc(root_ready, 1)
                elif step == "operand":
                    target = u_hi[(tail.sweep + 1) % 2]
                    if kind == MLP_U:
                        act.wait_ge(act_ready[2], e + 1)
                        source = act_n[:]
                    else:
                        act.wait_ge(normed, norm_tail + 1)
                        source = normed_n[:]
                    if kind in (MLP_U, CONV_2):
                        nc.scalar.activation(target[:, cols(tail.out)], source, ACT.Copy).then_inc(u_hi_ready, 1)
                        return
                    act.wait_ge(scale_in_ready, norm_tail + 1)
                    for c in range(TILES):
                        done = nc.scalar.activation(target[:, ds(tail.out * BLOCK + c * P, P)], normed_n[:, tile(c)],
                                                    ACT.Copy, scale=scale_in[:, c:c + 1])
                    done.then_inc(u_hi_ready, 1)

            def load_constants():
                act.dma_start(b_mlp[:], mlp_biases).then_inc(constants_loaded, 16)
                act.dma_start(w[:], weights).then_inc(constants_loaded, 16)
                act.dma_start(ident[:], constants).then_inc(constants_loaded, 16)
                act.dma_start(partial[0:ROWS, 0:2 * BLOCK], last_biases.partition_broadcast(ROWS))\
                   .then_inc(constants_loaded, 16)
                for k in range(TILES + 1):
                    act.dma_start(b_conv[:, k, :], conv_biases[k // TILES, :].partition_broadcast(P))\
                       .then_inc(constants_loaded, 16)

            def split_turn(turn):
                order = ("scale_out", "scale_in", "leaky1", "leaky2", "leaky3", "root", "operand")
                for k in range(LEAD, turn.granules + LEAD + 1):
                    for tail, step in steps_at(turn, split_places, order, k):
                        tail_step(tail, step)
                    if has_own(turn) and k == (FRESH_OWN if turn.fresh else OWN):
                        act.wait_ge(granule_used, turn.granule0)
                        if turn.fresh:
                            act.wait_ge(u_ready, turn.n + 1)
                        here = turn.group.sweep % 2
                        nc.scalar.activation(own_hi[:], u_hi[here][:, cols(turn.out)].bitcast(f32), ACT.Copy)
                        nc.scalar.activation(own_lo[:], u_lo[here][:, cols(turn.out)].bitcast(f32),
                                             ACT.Copy).then_inc(own_ready, 1)
                    if isinstance(turn.n, int) and turn.n == 0 and k < turn.granules and k % GRANULES_PER_BLOCK == 0:
                        split_x(k // GRANULES_PER_BLOCK)
                    if turn.group.shared and k == turn.granules + LEAD - GRANULES_PER_BLOCK + 1:
                        act.wait_ge(acc_done, part_turn(turn) + 1)
                        nc.scalar.activation(out_t[:], bank_of(acc, turn.n), ACT.Copy).then_inc(evacuated, 1)
                    if isinstance(turn.n, int) and turn.n == 0 and k == turn.granules:
                        act.wait_ge(constants_loaded, CONSTANTS)
                        nc.scalar.activation(ident_r[:], ident[:], ACT.Copy)
                        nc.scalar.activation(b_last[:], partial[0:ROWS, 0:2 * BLOCK],
                                             ACT.Copy).then_inc(constants_hi, 1)
                    if k < turn.granules + (0 if turn.last else LEAD):
                        granule(turn, k)
                if not (turn.group.adds_partial or turn.group.shared):
                    act.wait_ge(granule_used, turn.granule0 + turn.granules)
                    nc.scalar.activation(out_t[:], bank_of(acc, turn.n), ACT.Copy).then_inc(evacuated, 1)
                if turn.group.shared:
                    act.wait_ge(granule_used, turn.granule0 + turn.granules)
                    nc.scalar.activation(partial[:, partial_cols(turn)], bank_of(part, turn.n),
                                         ACT.Copy).then_inc(part_free, 1)
                if isinstance(turn.n, int) and turn.n == DEGREE_TURN:
                    act.wait_ge(degree_safe_ready, 1)
                    nc.scalar.activation(degree_root[:], degree_safe[:], ACT.Sqrt).then_inc(degree_root_ready, 1)

            first = turn_of(GROUPS[0], 0)

            def split_x(c):
                act.wait_ge(x_loaded[c], 16)
                done = nc.scalar.activation(u_hi[0][:, c * BLOCK:(c + 1) * BLOCK],
                                            x_res[:, c * BLOCK:(c + 1) * BLOCK], ACT.Copy)
                done.then_inc(x_hi_ready, 1)

            for k in range(LEAD):
                if k % GRANULES_PER_BLOCK == 0:
                    split_x(k // GRANULES_PER_BLOCK)
                granule(first, k)
            load_constants()
            nc.scalar.activation(root[:], x_res[:, 0:TILES], ACT.Copy).then_inc(part_free, 2)
            run_turns(act, split_turn)
            finale, = turn_of(GROUPS[-1], HALF).tails
            for step in ("scale_out", "root"):
                tail_step(finale, step)

        @block.vector
        def _(dve):
            def granule(turn, k):
                number = turn.granule0 + k
                slot = (k // GRANULES_PER_BLOCK) % RAW_SLOTS
                start = (k % GRANULES_PER_BLOCK) * GRANULE
                dve.wait_ge(hi_done, number + 1)
                nc.vector.tensor_tensor(mat_lo[:, k % SPLIT_SLOTS, :], raw[:, slot, start:start + GRANULE],
                                        mat_hi[:, k % SPLIT_SLOTS, :].bitcast(f32),
                                        ALU.subtract).then_inc(lo_done, 1)
                if is_counted(turn, k):
                    g = turn.group
                    adds_before = (before(g, lambda q: len(q.counted) * TILES)
                                   + turn.i * len(g.counted) * TILES
                                   + sorted(g.counted).index(k // GRANULES_PER_BLOCK) * TILES
                                   + (k % GRANULES_PER_BLOCK) * GRANULE_TILES)
                    for t in range(GRANULE_TILES):
                        dve.wait_ge(row_added, adds_before + t + 1)
                        nc.vector.tensor_tensor(row_sums[:, cols(turn.out)], row_sums[:, cols(turn.out)],
                                                raw[:, slot, start + t * BLOCK:start + (t + 1) * BLOCK],
                                                ALU.add).then_inc(row_added, 1)

            def tail_step(tail, step, count):
                e, kind, where = tail.n, tail.kind, tail.out
                norm_tail = e - FIRST_NORMED
                there = (tail.sweep + 1) % 2

                def signalled(instruction):
                    count[0] += 1
                    instruction.then_inc(vector_step, 1)

                def wait_own():
                    dve.wait_ge(vector_step, vector_steps_before(tail) + count[0])

                if step in ("leaky1", "leaky2"):
                    k = int(step[-1]) - 1
                    dve.wait_ge(pre_ready[k], e + 1)
                    nc.vector.scalar_tensor_tensor(act_t[:], pre_t[:], LEAK, pre_t[:], ALU.mult,
                                                   ALU.max).then_inc(act_ready[k], 1)
                elif step == "leaky3":
                    dve.wait_ge(pre_ready[2], e + 1)
                    nc.vector.scalar_tensor_tensor(act_n[:], pre_t[:], LEAK, pre_t[:], ALU.mult,
                                                   ALU.max).then_inc(act_ready[2], 1)
                elif step == "sum":
                    x_here = x_res[:, cols(where)]
                    if kind != MLP_LAST:
                        dve.wait_ge(natural_done, e + 1)
                        dve.wait_ge(saved, norm_tail + 1)
                    if kind == MLP_LAST:
                        dve.wait_ge(act_ready[2], e + 1)
                        signalled(nc.vector.tensor_tensor(sum_n[:], act_n[:], x_here, ALU.add))
                    elif kind in (CONV_1, CONV_2):
                        dve.wait_ge(scale_out_ready, e - FIRST_SCALED + 1)
                        if kind == CONV_1:
                            dve.wait_ge(x_bias_ready, e - FIRST_SCALED + 1)
                        for c in range(TILES):
                            signalled(nc.vector.scalar_tensor_tensor(
                                sum_n[:, tile(c)], natural[:, tile(c)], scale_out[:, c:c + 1],
                                x_bias[:, tile(c)] if kind == CONV_1 else b_conv[:, TILES, :],
                                ALU.mult, ALU.add))
                        if kind == CONV_2:
                            wait_own()
                            signalled(nc.vector.scalar_tensor_tensor(sum_n[:], sum_n[:], 0.0, x_here,
                                                                     ALU.max, ALU.add))
                    else:
                        dve.wait_ge(scale_out_ready, e - FIRST_SCALED + 1)
                        for c in range(TILES):
                            signalled(nc.vector.scalar_tensor_tensor(
                                sum_n[:, tile(c)], natural[:, tile(c)], scale_out[:, c:c + 1],
                                x_res[:, ds(where * BLOCK + c * P, P)], ALU.mult, ALU.add))
                elif step == "moments":
                    wait_own()
                    for c in range(TILES):
                        signalled(nc.vector.bn_stats(stats[:, c, :], sum_n[:, tile(c)]))
                    wait_own()
                    nc.vector.memset(wait_carrier[:], 0.0)
                    for c in range(TILES):
                        signalled(nc.vector.bn_aggr(moments[:, c, :], stats[:, c, :]))
                    wait_own()
                    nc.vector.tensor_scalar(var_eps[:], moments[:, :, 1], LN_EPS, None,
                                            ALU.add).then_inc(var_ready, 1)
                elif step == "norm":
                    dve.wait_ge(root_ready, norm_tail + 1)
                    signalled(nc.vector.reciprocal(inv_root[:], root[:]))
                    wait_own()
                    signalled(nc.vector.scalar_tensor_tensor(newton[:], var_eps[:], 0.5, inv_root[:],
                                                             ALU.mult, ALU.mult))
                    wait_own()
                    signalled(nc.vector.scalar_tensor_tensor(better_root[:], root[:], 0.5, newton[:],
                                                             ALU.mult, ALU.add))
                    wait_own()
                    dve.wait_ge(saved, norm_tail + 1)
                    rstd_made = nc.vector.reciprocal(rstd[:], better_root[:])
                    rstd_made.then_inc(rstd_ready, 1)
                elif step == "normalise":
                    dve.wait_ge(rstd_ready, norm_tail + 1)
                    for c in range(TILES):
                        done = nc.vector.tensor_scalar(normed_n[:, tile(c)], sum_n[:, tile(c)],
                                                       moments[:, c, 0:1], rstd[:, c:c + 1],
                                                       ALU.subtract, ALU.mult)
                    done.then_inc(normed, 1)
                    assert count[0] == VECTOR_STEPS[kind], (kind, count[0])
                elif step == "operand":
                    dve.wait_ge(u_hi_ready, e + 1)
                    high, low = u_hi[there], u_lo[there]
                    if kind in (MLP_U, CONV_2):
                        source = act_n if kind == MLP_U else normed_n
                        nc.vector.tensor_tensor(low[:, cols(where)], source[:], high[:, cols(where)].bitcast(f32),
                                                ALU.subtract).then_inc(u_ready, 1)
                        return
                    dve.wait_ge(scale_in_ready, norm_tail + 1)
                    for c in range(TILES):
                        here = ds(where * BLOCK + c * P, P)
                        done = nc.vector.scalar_tensor_tensor(low[:, here], normed_n[:, tile(c)], scale_in[:, c:c + 1],
                                                              high[:, here].bitcast(f32), ALU.mult, ALU.subtract)
                    done.then_inc(u_ready, 1)

            def chained(instruction, steps):
                steps[0] += 1
                instruction.then_inc(degree_step, 1)
                dve.wait_ge(degree_step, steps[0])

            degree_steps = [0]

            def row_degrees():
                steps = degree_steps
                dve.wait_ge(degree_summed, 1)
                chained(nc.vector.tensor_scalar(degree[:], degree_sums[:, 0:NODE_TILES], 1.0, None, ALU.add), steps)
                chained(nc.vector.tensor_scalar(is_zero[:], degree[:], 0.0, None, ALU.is_equal), steps)
                nc.vector.tensor_tensor(degree_safe[:], degree[:], is_zero[:], ALU.add)\
                  .then_inc(degree_safe_ready, 1)
                chained(nc.vector.tensor_scalar(not_zero[:], is_zero[:], -1.0, 1.0, ALU.mult, ALU.add), steps)
                dve.wait_ge(degree_root_ready, 1)
                chained(nc.vector.reciprocal(degree_inv[:], degree_root[:]), steps)
                chained(nc.vector.scalar_tensor_tensor(degree_work[:], degree_safe[:], 0.5, degree_inv[:],
                                                       ALU.mult, ALU.mult), steps)
                chained(nc.vector.scalar_tensor_tensor(degree_better[:], degree_root[:], 0.5, degree_work[:],
                                                       ALU.mult, ALU.add), steps)
                chained(nc.vector.tensor_tensor(root_or_zero[:], degree_better[:], not_zero[:], ALU.mult), steps)
                chained(nc.vector.reciprocal(conv2_scale[:], root_or_zero[:]), steps)
                chained(nc.vector.reciprocal(degree_inv[:], degree_better[:]), steps)
                nc.vector.tensor_tensor(conv1_scale[:], degree_inv[:], not_zero[:], ALU.mult)\
                  .then_inc(degrees_ready, 1)

            def column_degrees():
                steps = degree_steps
                chained(nc.vector.tensor_reduce(col_sum[:], col_sums[:], AX.X, ALU.add), steps)
                chained(nc.vector.tensor_scalar(col_zero[:], col_sum[:], 0.0, None, ALU.is_equal), steps)
                chained(nc.vector.tensor_tensor(col_safe[:], col_sum[:], col_zero[:], ALU.add), steps)
                chained(nc.vector.tensor_scalar(col_not[:], col_zero[:], -1.0, 1.0, ALU.mult, ALU.add), steps)
                chained(nc.vector.reciprocal(col_inv[:], col_safe[:]), steps)
                chained(nc.vector.tensor_tensor(hyper_scale[:], col_inv[:], col_not[:], ALU.mult), steps)

            def split_turn(turn):
                order = ("leaky1", "leaky2", "leaky3", "sum", "moments", "norm", "normalise", "operand")
                counts = {tail.stage: [0] for tail in turn.tails}
                for k in range(LEAD, turn.granules + LEAD + 1):
                    for tail, step in steps_at(turn, split_places, order, k):
                        tail_step(tail, step, counts[tail.stage])
                    if isinstance(turn.n, int) and turn.n == 0 and k < turn.granules and k % GRANULES_PER_BLOCK == 0:
                        split_x(k // GRANULES_PER_BLOCK)
                    if isinstance(turn.n, int) and turn.n == 0 and k == turn.granules:
                        dve.wait_ge(constants_hi, 1)
                        nc.vector.tensor_tensor(b_last[LO_ROW:ROWS, :], partial[LO_ROW:ROWS, 0:2 * BLOCK],
                                                b_last[LO_ROW:ROWS, :].bitcast(f32),
                                                ALU.subtract).then_inc(constants_ready, 1)
                    if k < turn.granules + (0 if turn.last else LEAD):
                        granule(turn, k)
                if turn.group.adds_partial:
                    dve.wait_ge(granule_used, turn.granule0 + turn.granules)
                    nc.vector.tensor_tensor(out_t[:], bank_of(acc, turn.n), partial[:, partial_cols(turn)],
                                            ALU.add).then_inc(evacuated, 1)
                if isinstance(turn.n, int) and turn.n == DEGREE_TURN:
                    row_degrees()
                if isinstance(turn.n, int) and turn.n == DEGREE_TURN + HALF:
                    column_degrees()

            first = turn_of(GROUPS[0], 0)

            def split_x(c):
                dve.wait_ge(x_hi_ready, c + 1)
                here = slice(c * BLOCK, (c + 1) * BLOCK)
                nc.vector.tensor_tensor(u_lo[0][:, here], x_res[:, here], u_hi[0][:, here].bitcast(f32),
                                        ALU.subtract).then_inc(x_split, 1)
                if c == BLOCKS - 1:
                    dve.wait_ge(x_split, BLOCKS)
                    nc.vector.memset(inv_root[:], 0.0).then_inc(u_ready, 1)

            for k in range(LEAD):
                if k % GRANULES_PER_BLOCK == 0:
                    split_x(k // GRANULES_PER_BLOCK)
                granule(first, k)
            nc.vector.memset(newton[:], 0.0).then_inc(evacuated, 1)
            run_turns(dve, split_turn)
            finale, = turn_of(GROUPS[-1], HALF).tails
            count = [0]
            for step in ("sum", "moments", "norm", "normalise"):
                tail_step(finale, step, count)

        @block.tensor
        def _(pe):
            def tail_step(tail, step):
                e, kind = tail.n, tail.kind
                norm_tail = e - FIRST_NORMED
                if step in ("dense1", "dense2"):
                    k = int(step[-1]) - 1
                    if k == 0:
                        pe.wait_ge(evacuated, e + 2)
                    else:
                        pe.wait_ge(act_ready[k - 1], e + 1)
                    nc.tensor.matmul(dense[k][:], w[:, (tail.sweep % 2) * 3 + k, :], (act_t if k else out_t)[:],
                                     start=True, stop=True).then_inc(dense_done[k], 1)
                elif step == "natural":
                    if kind == MLP_U:
                        pe.wait_ge(u_ready, e + 1)
                    elif kind == MLP_LAST:
                        pe.wait_ge(act_ready[2], e)
                    else:
                        pe.wait_ge(normed, norm_tail)
                    if kind in (MLP_U, MLP_LAST):
                        mlp = tail.sweep % 2
                        nc.tensor.matmul(natural[:], ident_r[0:ROWS, P:2 * P], b_last[:, mlp * BLOCK:(mlp + 1) * BLOCK],
                                         start=True, stop=False)
                        pe.wait_ge(act_ready[1], e + 1)
                        for c in range(TILES):
                            done = nc.tensor.matmul(natural[:, tile(c)], act_t[:, tile(c)], w[:, mlp * 3 + 2, :],
                                                    start=False, stop=c == TILES - 1)
                        done.then_inc(natural_done, 1)
                        return
                    pe.wait_ge(evacuated, e + 2)
                    for c in range(TILES):
                        if kind == HYPER:
                            done = nc.tensor.transpose(natural[:, tile(c)], out_t[:, tile(c)], ident[:, 0:P])
                        else:
                            done = nc.tensor.matmul(natural[:, tile(c)], out_t[:, tile(c)],
                                                    w[:, 6 if kind == CONV_1 else 7, :], start=True, stop=True)
                    done.then_inc(natural_done, 1)

            def sum_degrees():
                counted = sum(HALF * TILES * len(g.counted) for g in GROUPS)
                assert counted == BLOCKS * NODE_TILES
                pe.wait_ge(row_added, counted + 1)
                pe.wait_ge(ones_set, 1)
                for t in range(NODE_TILES):
                    done = nc.tensor.matmul(degree_sums[:, t:t + 1], row_sums[:, tile(t)], ones[:],
                                            start=True, stop=True)
                done.then_inc(degree_summed, 1)

            def products(turn):
                group, n = turn.group, turn.n
                here, there = group.sweep % 2, (group.sweep + 1) % 2
                if not (isinstance(n, int) and n == 0):
                    pe.wait_ge(evacuated, n)
                    if turn.fresh:
                        pe.wait_ge(u_ready, n)
                if group.shared:
                    pe.wait_ge(part_free, part_turn(turn) + 1)
                acc_out, part_out = bank_of(acc, n), bank_of(part, n)
                last_place = len(blocks_of(group)) - 1

                def granule_products(k, for_part):
                    place = k // GRANULES_PER_BLOCK
                    first_place, parity, target = (1, there, part_out) if for_part else (0, here, acc_out)
                    last = k == turn.granules - 1
                    for t in range(GRANULE_TILES):
                        jt = (blocks_of(group)[place] * TILES
                              + (k % GRANULES_PER_BLOCK) * GRANULE_TILES + t)
                        start = place == first_place and k % GRANULES_PER_BLOCK == 0 and t == 0
                        stop = last and t == GRANULE_TILES - 1 and (for_part or not has_own(turn))
                        strip = slice(t * BLOCK, (t + 1) * BLOCK)
                        hi, lo = mat_hi[:, k % SPLIT_SLOTS, strip], mat_lo[:, k % SPLIT_SLOTS, strip]
                        nc.tensor.matmul(target, u_hi[parity][:, tile(jt)], hi, start=start, stop=False)
                        nc.tensor.matmul(target, u_hi[parity][:, tile(jt)], lo, start=False, stop=False)
                        done = nc.tensor.matmul(target, u_lo[parity][:, tile(jt)], hi, start=False, stop=stop)
                    if last and not for_part and has_own(turn):
                        pe.wait_ge(own_ready, n - FIRST_SCALED + 1)
                        for operand in (own_hi, own_lo):
                            for t in range(TILES):
                                done = nc.tensor.matmul(acc[:, ds((n & 1) * BLOCK + t * P, P)], operand[:, tile(t)],
                                                        ident_r[:, 0:P], start=False,
                                                        stop=operand is own_lo and t == TILES - 1)
                    return done

                order = ("dense1", "dense2", "natural")
                for tail, step in steps_at(turn, tensor_places, order, -1):
                    tail_step(tail, step)
                for k in range(turn.granules):
                    place = k // GRANULES_PER_BLOCK
                    shared = bool(group.shared) and place % 2 == 1
                    if k % GRANULES_PER_BLOCK == 0:
                        if isinstance(n, int) and n == 0:
                            pe.wait_ge(x_split, place + 1)
                        elif place == last_place and turn.fresh:
                            pe.wait_ge(u_ready, n + 1)
                    pe.wait_ge(lo_done, turn.granule0 + k + 1)
                    done = granule_products(k, False)
                    if shared and place == last_place:
                        if k == turn.granules - 1:
                            done.then_inc(acc_done, 1)
                            pe.wait_ge(u_ready, n + 1)
                            for waiting in range(turn.granules - GRANULES_PER_BLOCK, turn.granules):
                                granule_products(waiting, True).then_inc(granule_used, 1)
                    else:
                        if shared:
                            done = granule_products(k, True)
                        done.then_inc(granule_used, 1)
                    if isinstance(n, int) and n == 0 and k == turn.granules - 1:
                        pe.wait_ge(constants_ready, 1)
                    for tail, step in steps_at(turn, tensor_places, order, k):
                        tail_step(tail, step)
                    if k == DEGREE_PLACE and isinstance(n, int) and n == DEGREE_TURN:
                        sum_degrees()

            run_turns(pe, products)
            tail_step(turn_of(GROUPS[-1], HALF).tails[0], "natural")


def kernel(x, adj, L0_gnn_v_node_feats, L0_gnn_uv_W1, L0_gnn_uv_b1, L0_gnn_uv_W2, L0_gnn_uv_b2,
           L0_gnn_uv_W3, L0_gnn_uv_b3, L0_gnn_vu_W1, L0_gnn_vu_b1, L0_gnn_vu_W2, L0_gnn_vu_b2,
           L0_gnn_vu_W3, L0_gnn_vu_b3, L1_gnn_W, L1_gnn_b, L2_gnn_W, L2_gnn_b):
    import numpy as np
    import concourse.bacc as bacc
    from concourse.bass_utils import run_bass_kernel_spmd

    a, x = np.asarray(adj), np.asarray(x)
    strip = (-1, P, TILES * BLOCK)
    two_rows = np.zeros((P, P), np.float32)
    two_rows[[0, LO_ROW]] = 1
    arrays = {
        "stream": np.concatenate([
            x.reshape(ADJ_T, -1, P, FEATURES).transpose(0, 2, 1, 3).reshape(strip),
            a.reshape(BLOCKS, BLOCK, BLOCKS, TILES, P).transpose(0, 2, 4, 3, 1).reshape(strip),
            a.reshape(BLOCKS, TILES, P, BLOCKS, BLOCK).transpose(3, 0, 2, 1, 4).reshape(strip)]),
        "weights": np.stack([np.asarray(m) for m in (
            L0_gnn_uv_W1, L0_gnn_uv_W2, L0_gnn_uv_W3, L0_gnn_vu_W1, L0_gnn_vu_W2, L0_gnn_vu_W3,
            np.asarray(L1_gnn_W).T, L2_gnn_W)], axis=1),
        "mlp_biases": np.stack([np.asarray(b) for b in (
            L0_gnn_uv_b1, L0_gnn_uv_b2, L0_gnn_vu_b1, L0_gnn_vu_b2)], axis=1),
        "last_biases": np.concatenate([np.tile(np.asarray(b), TILES) for b in (L0_gnn_uv_b3, L0_gnn_vu_b3)]),
        "conv_biases": np.stack([np.asarray(L1_gnn_b), np.asarray(L2_gnn_b)]),
        "constants": np.concatenate([np.eye(P, dtype=np.float32), two_rows], axis=1),
    }
    arrays = {name: np.ascontiguousarray(value) for name, value in arrays.items()}
    nc = bacc.Bacc("TRN2", target_bir_lowering=False, num_devices=1)
    args = [nc.dram_tensor(name, v.shape, mybir.dt.from_np(v.dtype), kind="ExternalInput").ap()
            for name, v in arrays.items()]
    out = nc.dram_tensor("out_blocks", (BLOCKS, P, BLOCK), mybir.dt.float32, kind="ExternalOutput").ap()
    gnn_stack(nc, *args, out)
    got = run_bass_kernel_spmd(nc, [arrays], core_ids=[0]).results[0]["out_blocks"]
    return got.reshape(BLOCKS, P, TILES, FEATURES).transpose(0, 2, 1, 3).reshape(NODES, FEATURES)
```
